# Optimizing a Trainium2 kernel written in Bass

```python
import numpy as np
import jax
import jax.numpy as jnp

def _softmax(x, axis=-1):
    return jax.nn.softmax(x, axis=axis)

def _gelu(x):
    return jax.nn.gelu(x, approximate=True)

def _silu(x):
    return jax.nn.silu(x)

def _sigmoid(x):
    return jax.nn.sigmoid(x)

def _layernorm(x, axis=-1, eps=1e-05):
    m = jnp.mean(x, axis=axis, keepdims=True)
    v = jnp.var(x, axis=axis, keepdims=True)
    return (x - m) / jnp.sqrt(v + eps)

def _scatter_add(tgt, idx, src, axis=0):
    return tgt.at[idx].add(src)

def _segment_sum(src, seg, n):
    return jax.ops.segment_sum(src, seg, n)
kernel_name = 'mk_hybrid_d1_jaxref_r8_2d2a67'

def setup_inputs(seed: int=0):
    np.random.seed(seed)
    _w = jnp.asarray

    def _L0_attn_a_setup():
        import jax, jax.numpy as jnp
        import numpy as np
        import math
        B, S, E, H = (2, 256, 128, 16)
        D = E // H
        SCALE = 1.0 / math.sqrt(D)
        key = jax.random.key(seed)
        ks = jax.random.split(key, 5)
        std = 0.02
        return {'q': jax.random.normal(ks[0], (B, S, E), dtype=jnp.float32), 'Wq': jax.random.normal(ks[1], (E, H * D), dtype=jnp.float32) * std, 'Wk': jax.random.normal(ks[2], (E, H * D), dtype=jnp.float32) * std, 'Wv': jax.random.normal(ks[3], (E, H * D), dtype=jnp.float32) * std, 'Wo': jax.random.normal(ks[4], (H * D, E), dtype=jnp.float32) * std, 'gamma': jnp.ones((H,), dtype=jnp.float32)}
    _L0_attn_a_in = _L0_attn_a_setup()

    def _L0_attn_b_setup():
        import jax, jax.numpy as jnp
        import numpy as np
        BATCH, L, H, P = (4, 1024, 128, 32)
        EPS = 1e-06

        def _reference_tuple_inner(hidden_states, norm_weight, Lambda_re, Lambda_im, log_step, B_re, B_im, C_re, C_im, D):
            ms = jnp.mean(hidden_states * hidden_states, axis=-1, keepdims=True)
            u = hidden_states * jax.lax.rsqrt(ms + EPS) * norm_weight
            Lam = Lambda_re + 1j * Lambda_im
            dt = jnp.exp(log_step)
            Lam_bar = jnp.exp(Lam * dt)
            B_bar = ((Lam_bar - 1.0) / Lam)[:, None] * (B_re + 1j * B_im)
            Bu = jnp.einsum('blh,ph->blp', u, jnp.real(B_bar)) + 1j * jnp.einsum('blh,ph->blp', u, jnp.imag(B_bar))
            As = jnp.broadcast_to(Lam_bar.astype(Bu.dtype), Bu.shape)

            def op(e1, e2):
                a1, b1 = e1
                a2, b2 = e2
                return (a2 * a1, a2 * b1 + b2)
            _, xs = jax.lax.associative_scan(op, (As, Bu), axis=1)
            y = 2.0 * (jnp.einsum('blp,hp->blh', jnp.real(xs), C_re) - jnp.einsum('blp,hp->blh', jnp.imag(xs), C_im)) + D * u
            out = hidden_states + y
            final_state = xs[:, -1]
            return (out, final_state)
        key = jax.random.key(seed)
        ks = jax.random.split(key, 8)
        hidden_states = jax.random.normal(ks[0], (BATCH, L, H), jnp.float32)
        norm_weight = jnp.ones((H,), jnp.float32)
        Lambda_re = -0.5 * jnp.ones((P,), jnp.float32)
        Lambda_im = jnp.pi * jnp.arange(P, dtype=jnp.float32)
        log_step = jax.random.uniform(ks[1], (P,), jnp.float32) * (np.log(0.1) - np.log(0.001)) + np.log(0.001)
        B_re = jax.random.normal(ks[2], (P, H), jnp.float32) / np.sqrt(H)
        B_im = jax.random.normal(ks[3], (P, H), jnp.float32) / np.sqrt(H)
        C_re = jax.random.normal(ks[4], (H, P), jnp.float32) / np.sqrt(P)
        C_im = jax.random.normal(ks[5], (H, P), jnp.float32) / np.sqrt(P)
        D = jax.random.normal(ks[6], (H,), jnp.float32)
        return {'hidden_states': hidden_states, 'norm_weight': norm_weight, 'Lambda_re': Lambda_re, 'Lambda_im': Lambda_im, 'log_step': log_step, 'B_re': B_re, 'B_im': B_im, 'C_re': C_re, 'C_im': C_im, 'D': D}
    _L0_attn_b_in = _L0_attn_b_setup()

    def _L0_ffn_setup():
        import jax, jax.numpy as jnp
        import numpy as np
        DIM = 128
        H = 8
        DH = 64
        W = 64
        NQ = 64
        NKV = 128
        EPS = 1.0
        NITERS = 50
        FETCH = 9.0 / 8.0
        SCALE = DH ** (-0.5)

        def _ln(x, w, b):
            m = x.mean(-1, keepdims=True)
            v = ((x - m) ** 2).mean(-1, keepdims=True)
            return (x - m) * jax.lax.rsqrt(v + 1e-05) * w + b

        def _rms(x, g):
            n = jnp.maximum(jnp.linalg.norm(x, axis=-1, keepdims=True), 1e-12)
            return x / n * np.sqrt(DIM).astype(np.float32) * g

        def local_attn(x, Wqkv, Wout):
            b, n, _ = x.shape
            nw = n // W
            qkv = x @ Wqkv.T
            q, k, v = jnp.split(qkv, 3, axis=-1)

            def towin(t):
                return t.reshape(b, nw, W, H, DH).transpose(0, 3, 1, 2, 4)
            q, k, v = map(towin, (q, k, v))

            def expand(t):
                tp = jnp.pad(t, ((0, 0), (0, 0), (1, 1), (0, 0), (0, 0)))
                return jnp.concatenate([tp[:, :, :-2], tp[:, :, 1:-1], tp[:, :, 2:]], axis=3)
            ke, ve = (expand(k), expand(v))
            sim = jnp.einsum('bhnid,bhnjd->bhnij', q, ke) * SCALE
            win = jnp.arange(nw)
            valid = jnp.concatenate([jnp.repeat((win > 0)[:, None], W, 1), jnp.ones((nw, W), bool), jnp.repeat((win < nw - 1)[:, None], W, 1)], axis=1)
            sim = jnp.where(valid[None, None, :, None, :], sim, -1000000000.0)
            attn = jax.nn.softmax(sim, axis=-1)
            o = jnp.einsum('bhnij,bhnjd->bhnid', attn, ve)
            o = o.transpose(0, 2, 3, 1, 4).reshape(b, n, H * DH)
            return o @ Wout.T

        def route(x, routing_token, num_tokens):
            s = jnp.einsum('bnd,rd->brn', x, routing_token).reshape(x.shape[0], x.shape[1])
            n = s.shape[-1]
            logk = jnp.log(jnp.asarray(min(num_tokens * FETCH, float(n)), s.dtype))

            def body(ab, _):
                a, bb = ab
                a = EPS * (logk - jax.nn.logsumexp((s + bb) / EPS, axis=-1, keepdims=True))
                bb = -jax.nn.relu(s + a)
                return ((a, bb), None)
            (a, bb), _ = jax.lax.scan(body, (jnp.zeros((s.shape[0], 1), s.dtype), -s), None, length=NITERS)
            scores = jnp.exp((s + a + bb) / EPS)
            sel_scores, sel_idx = jax.lax.top_k(scores, num_tokens)
            sel_scores = sel_scores + jax.lax.stop_gradient(1.0 - sel_scores)
            return (sel_scores, sel_idx)

        def heavy_attn(xq, ctx, scores_kv, gamma, Wq, Wkv, Wout, null_kv):
            b = xq.shape[0]
            xq = _rms(xq, gamma)
            ctx = _rms(ctx, gamma)
            q = (xq @ Wq.T).reshape(b, -1, H, DH).transpose(0, 2, 1, 3)
            kv = (ctx @ Wkv.T).reshape(b, -1, H, 2 * DH).transpose(0, 2, 1, 3)
            k, v = (kv[..., :DH], kv[..., DH:])
            v = v * scores_kv[:, None, :, None]
            nk = jnp.broadcast_to(null_kv[0][None, :, None, :], (b, H, 1, DH))
            nv = jnp.broadcast_to(null_kv[1][None, :, None, :], (b, H, 1, DH))
            k = jnp.concatenate([nk, k], axis=2)
            v = jnp.concatenate([nv, v], axis=2)
            sim = jnp.einsum('bhid,bhjd->bhij', q, k) * SCALE
            attn = jax.nn.softmax(sim, axis=-1)
            o = jnp.einsum('bhij,bhjd->bhid', attn, v)
            o = o.transpose(0, 2, 1, 3).reshape(b, -1, H * DH)
            return o @ Wout.T
        key = jax.random.key(seed)
        ks = jax.random.split(key, 12)
        D, IN = (DIM, H * DH)
        w = lambda k, shape: jax.random.normal(k, shape, jnp.float32) * 0.02
        return {'x': jax.random.normal(ks[0], (4, 512, D), jnp.float32), 'ln_w': jnp.ones((D,), jnp.float32), 'ln_b': jnp.zeros((D,), jnp.float32), 'Wqkv': w(ks[1], (3 * IN, D)), 'Wout_l': w(ks[2], (D, IN)), 'rt_q': jax.random.normal(ks[3], (1, D), jnp.float32), 'rt_kv': jax.random.normal(ks[4], (1, D), jnp.float32), 'gamma': jnp.ones((D,), jnp.float32), 'Wq': w(ks[5], (IN, D)), 'Wkv': w(ks[6], (2 * IN, D)), 'Wout_h': w(ks[7], (D, IN)), 'null_kv': jax.random.normal(ks[8], (2, H, DH), jnp.float32), 'null_q': jax.random.normal(ks[9], (D,), jnp.float32)}
    _L0_ffn_in = _L0_ffn_setup()
    _d = {'L0_attn_a_q': _L0_attn_a_in['q'], 'L0_attn_a_Wq': _L0_attn_a_in['Wq'], 'L0_attn_a_Wk': _L0_attn_a_in['Wk'], 'L0_attn_a_Wv': _L0_attn_a_in['Wv'], 'L0_attn_a_Wo': _L0_attn_a_in['Wo'], 'L0_attn_a_gamma': _L0_attn_a_in['gamma'], 'L0_attn_b_norm_weight': _L0_attn_b_in['norm_weight'], 'L0_attn_b_Lambda_re': _L0_attn_b_in['Lambda_re'], 'L0_attn_b_Lambda_im': _L0_attn_b_in['Lambda_im'], 'L0_attn_b_log_step': _L0_attn_b_in['log_step'], 'L0_attn_b_B_re': _L0_attn_b_in['B_re'], 'L0_attn_b_B_im': _L0_attn_b_in['B_im'], 'L0_attn_b_C_re': _L0_attn_b_in['C_re'], 'L0_attn_b_C_im': _L0_attn_b_in['C_im'], 'L0_attn_b_D': _L0_attn_b_in['D'], 'L0_ffn_ln_w': _L0_ffn_in['ln_w'], 'L0_ffn_ln_b': _L0_ffn_in['ln_b'], 'L0_ffn_Wqkv': _L0_ffn_in['Wqkv'], 'L0_ffn_Wout_l': _L0_ffn_in['Wout_l'], 'L0_ffn_rt_q': _L0_ffn_in['rt_q'], 'L0_ffn_rt_kv': _L0_ffn_in['rt_kv'], 'L0_ffn_gamma': _L0_ffn_in['gamma'], 'L0_ffn_Wq': _L0_ffn_in['Wq'], 'L0_ffn_Wkv': _L0_ffn_in['Wkv'], 'L0_ffn_Wout_h': _L0_ffn_in['Wout_h'], 'L0_ffn_null_kv': _L0_ffn_in['null_kv'], 'L0_ffn_null_q': _L0_ffn_in['null_q']}
    _x0 = _d['L0_attn_a_q']
    _d['L0_attn_a_q'] = jax.random.normal(jax.random.fold_in(jax.random.key(seed), 1), (16, 512, 128), dtype=_x0.dtype)
    del _x0
    return _d

def reference(L0_attn_a_q, L0_attn_a_Wq, L0_attn_a_Wk, L0_attn_a_Wv, L0_attn_a_Wo, L0_attn_a_gamma, L0_attn_b_norm_weight, L0_attn_b_Lambda_re, L0_attn_b_Lambda_im, L0_attn_b_log_step, L0_attn_b_B_re, L0_attn_b_B_im, L0_attn_b_C_re, L0_attn_b_C_im, L0_attn_b_D, L0_ffn_ln_w, L0_ffn_ln_b, L0_ffn_Wqkv, L0_ffn_Wout_l, L0_ffn_rt_q, L0_ffn_rt_kv, L0_ffn_gamma, L0_ffn_Wq, L0_ffn_Wkv, L0_ffn_Wout_h, L0_ffn_null_kv, L0_ffn_null_q):

    def _L0_attn_a_ref(q, Wq, Wk, Wv, Wo, gamma):
        import jax, jax.numpy as jnp
        import numpy as np
        import math
        B, S, E, H = (2, 256, 128, 16)
        D = E // H
        SCALE = 1.0 / math.sqrt(D)
        Bq, Sq, _ = q.shape
        qh = (q @ Wq).reshape(Bq, Sq, H, D).transpose(0, 2, 1, 3)
        kh = (q @ Wk).reshape(Bq, Sq, H, D).transpose(0, 2, 1, 3)
        vh = (q @ Wv).reshape(Bq, Sq, H, D).transpose(0, 2, 1, 3)
        q_norm = jnp.sum(qh * qh, axis=-1, keepdims=True)
        k_norm = jnp.sum(kh * kh, axis=-1, keepdims=True)
        qk = jnp.einsum('bhsd,bhtd->bhst', qh, kh)
        dist = jnp.maximum(q_norm - 2.0 * qk + jnp.swapaxes(k_norm, -2, -1), 0.0)
        scores = jnp.exp(-gamma[None, :, None, None] * SCALE * dist)
        mask = jnp.triu(jnp.ones((Sq, Sq), dtype=bool), k=1)
        scores = jnp.where(mask, scores, 0.0)
        out = jnp.einsum('bhst,bhtd->bhsd', scores, vh)
        out = out.transpose(0, 2, 1, 3).reshape(Bq, Sq, H * D)
        return out @ Wo

    def _L0_attn_b_ref(hidden_states, norm_weight, Lambda_re, Lambda_im, log_step, B_re, B_im, C_re, C_im, D):
        import jax, jax.numpy as jnp
        import numpy as np
        BATCH, L, H, P = (4, 1024, 128, 32)
        EPS = 1e-06

        def _reference_tuple_inner(hidden_states, norm_weight, Lambda_re, Lambda_im, log_step, B_re, B_im, C_re, C_im, D):
            ms = jnp.mean(hidden_states * hidden_states, axis=-1, keepdims=True)
            u = hidden_states * jax.lax.rsqrt(ms + EPS) * norm_weight
            Lam = Lambda_re + 1j * Lambda_im
            dt = jnp.exp(log_step)
            Lam_bar = jnp.exp(Lam * dt)
            B_bar = ((Lam_bar - 1.0) / Lam)[:, None] * (B_re + 1j * B_im)
            Bu = jnp.einsum('blh,ph->blp', u, jnp.real(B_bar)) + 1j * jnp.einsum('blh,ph->blp', u, jnp.imag(B_bar))
            As = jnp.broadcast_to(Lam_bar.astype(Bu.dtype), Bu.shape)

            def op(e1, e2):
                a1, b1 = e1
                a2, b2 = e2
                return (a2 * a1, a2 * b1 + b2)
            _, xs = jax.lax.associative_scan(op, (As, Bu), axis=1)
            y = 2.0 * (jnp.einsum('blp,hp->blh', jnp.real(xs), C_re) - jnp.einsum('blp,hp->blh', jnp.imag(xs), C_im)) + D * u
            out = hidden_states + y
            final_state = xs[:, -1]
            return (out, final_state)
        return _reference_tuple_inner(hidden_states, norm_weight, Lambda_re, Lambda_im, log_step, B_re, B_im, C_re, C_im, D)[0]

    def _L0_ffn_ref(x, ln_w, ln_b, Wqkv, Wout_l, rt_q, rt_kv, gamma, Wq, Wkv, Wout_h, null_kv, null_q):
        import jax, jax.numpy as jnp
        import numpy as np
        DIM = 128
        H = 8
        DH = 64
        W = 64
        NQ = 64
        NKV = 128
        EPS = 1.0
        NITERS = 50
        FETCH = 9.0 / 8.0
        SCALE = DH ** (-0.5)

        def _ln(x, w, b):
            m = x.mean(-1, keepdims=True)
            v = ((x - m) ** 2).mean(-1, keepdims=True)
            return (x - m) * jax.lax.rsqrt(v + 1e-05) * w + b

        def _rms(x, g):
            n = jnp.maximum(jnp.linalg.norm(x, axis=-1, keepdims=True), 1e-12)
            return x / n * np.sqrt(DIM).astype(np.float32) * g

        def local_attn(x, Wqkv, Wout):
            b, n, _ = x.shape
            nw = n // W
            qkv = x @ Wqkv.T
            q, k, v = jnp.split(qkv, 3, axis=-1)

            def towin(t):
                return t.reshape(b, nw, W, H, DH).transpose(0, 3, 1, 2, 4)
            q, k, v = map(towin, (q, k, v))

            def expand(t):
                tp = jnp.pad(t, ((0, 0), (0, 0), (1, 1), (0, 0), (0, 0)))
                return jnp.concatenate([tp[:, :, :-2], tp[:, :, 1:-1], tp[:, :, 2:]], axis=3)
            ke, ve = (expand(k), expand(v))
            sim = jnp.einsum('bhnid,bhnjd->bhnij', q, ke) * SCALE
            win = jnp.arange(nw)
            valid = jnp.concatenate([jnp.repeat((win > 0)[:, None], W, 1), jnp.ones((nw, W), bool), jnp.repeat((win < nw - 1)[:, None], W, 1)], axis=1)
            sim = jnp.where(valid[None, None, :, None, :], sim, -1000000000.0)
            attn = jax.nn.softmax(sim, axis=-1)
            o = jnp.einsum('bhnij,bhnjd->bhnid', attn, ve)
            o = o.transpose(0, 2, 3, 1, 4).reshape(b, n, H * DH)
            return o @ Wout.T

        def route(x, routing_token, num_tokens):
            s = jnp.einsum('bnd,rd->brn', x, routing_token).reshape(x.shape[0], x.shape[1])
            n = s.shape[-1]
            logk = jnp.log(jnp.asarray(min(num_tokens * FETCH, float(n)), s.dtype))

            def body(ab, _):
                a, bb = ab
                a = EPS * (logk - jax.nn.logsumexp((s + bb) / EPS, axis=-1, keepdims=True))
                bb = -jax.nn.relu(s + a)
                return ((a, bb), None)
            (a, bb), _ = jax.lax.scan(body, (jnp.zeros((s.shape[0], 1), s.dtype), -s), None, length=NITERS)
            scores = jnp.exp((s + a + bb) / EPS)
            sel_scores, sel_idx = jax.lax.top_k(scores, num_tokens)
            sel_scores = sel_scores + jax.lax.stop_gradient(1.0 - sel_scores)
            return (sel_scores, sel_idx)

        def heavy_attn(xq, ctx, scores_kv, gamma, Wq, Wkv, Wout, null_kv):
            b = xq.shape[0]
            xq = _rms(xq, gamma)
            ctx = _rms(ctx, gamma)
            q = (xq @ Wq.T).reshape(b, -1, H, DH).transpose(0, 2, 1, 3)
            kv = (ctx @ Wkv.T).reshape(b, -1, H, 2 * DH).transpose(0, 2, 1, 3)
            k, v = (kv[..., :DH], kv[..., DH:])
            v = v * scores_kv[:, None, :, None]
            nk = jnp.broadcast_to(null_kv[0][None, :, None, :], (b, H, 1, DH))
            nv = jnp.broadcast_to(null_kv[1][None, :, None, :], (b, H, 1, DH))
            k = jnp.concatenate([nk, k], axis=2)
            v = jnp.concatenate([nv, v], axis=2)
            sim = jnp.einsum('bhid,bhjd->bhij', q, k) * SCALE
            attn = jax.nn.softmax(sim, axis=-1)
            o = jnp.einsum('bhij,bhjd->bhid', attn, v)
            o = o.transpose(0, 2, 1, 3).reshape(b, -1, H * DH)
            return o @ Wout.T
        b, n, d = x.shape
        light = local_attn(_ln(x, ln_w, ln_b), Wqkv, Wout_l)
        sq, iq = route(x, rt_q, NQ)
        skv, ikv = route(x, rt_kv, NKV)
        br = jnp.arange(b)[:, None]
        xq = x[br, iq]
        xkv = x[br, ikv]
        heavy = heavy_attn(xq, xkv, skv, gamma, Wq, Wkv, Wout_h, null_kv)
        heavy = heavy * sq[..., None]
        out = jnp.broadcast_to(null_q[None, None, :], (b, n, d))
        out = out.at[br, iq].set(heavy)
        return out + light
    x = L0_attn_a_q
    x = x + _L0_attn_a_ref(_layernorm(x, axis=-1), L0_attn_a_Wq, L0_attn_a_Wk, L0_attn_a_Wv, L0_attn_a_Wo, L0_attn_a_gamma)
    x = x + _L0_ffn_ref(_layernorm(x, axis=-1), L0_ffn_ln_w, L0_ffn_ln_b, L0_ffn_Wqkv, L0_ffn_Wout_l, L0_ffn_rt_q, L0_ffn_rt_kv, L0_ffn_gamma, L0_ffn_Wq, L0_ffn_Wkv, L0_ffn_Wout_h, L0_ffn_null_kv, L0_ffn_null_q)
    x = x + _L0_attn_b_ref(_layernorm(x, axis=-1), L0_attn_b_norm_weight, L0_attn_b_Lambda_re, L0_attn_b_Lambda_im, L0_attn_b_log_step, L0_attn_b_B_re, L0_attn_b_B_im, L0_attn_b_C_re, L0_attn_b_C_im, L0_attn_b_D)
    x = x + _L0_ffn_ref(_layernorm(x, axis=-1), L0_ffn_ln_w, L0_ffn_ln_b, L0_ffn_Wqkv, L0_ffn_Wout_l, L0_ffn_rt_q, L0_ffn_rt_kv, L0_ffn_gamma, L0_ffn_Wq, L0_ffn_Wkv, L0_ffn_Wout_h, L0_ffn_null_kv, L0_ffn_null_q)
    return x

_drawn_inputs = setup_inputs


def setup_inputs(seed=0):
    import zlib

    import numpy as np

    out = dict(_drawn_inputs(seed))
    spreads = {'L0_attn_a_gamma': (1.0, 0.2),
     'L0_attn_b_norm_weight': (1.0, 0.2),
     'L0_attn_b_Lambda_re': (-0.5, 0.6),
     'L0_ffn_ln_w': (1.0, 0.6),
     'L0_ffn_ln_b': (0.0, 0.8),
     'L0_ffn_gamma': (1.0, 0.6)}
    factors = {'L0_ffn_rt_kv': 7.216,
     'L0_ffn_Wq': 8.0,
     'L0_ffn_Wkv': 3.144,
     'L0_ffn_Wout_h': 3.532,
     'L0_ffn_null_kv': 8.0}
    for name, (base, spread) in spreads.items():
        noise = np.random.default_rng([zlib.crc32(name.encode()), seed]).standard_normal(out[name].shape)
        drawn = base * np.exp(spread * noise) if base else spread * noise
        out[name] = jnp.asarray(drawn.astype(out[name].dtype))
    for name, factor in factors.items():
        out[name] = (out[name] * factor).astype(out[name].dtype)
    return out
```

```python
from contextlib import ExitStack

import numpy as np

import concourse.bass as bass
from concourse import mybir

F32 = mybir.dt.float32
BF16 = mybir.dt.bfloat16
ALU = mybir.AluOpType
ACT = mybir.ActivationFunctionType
AX = mybir.AxisListType.X

P = 128
B, S, E = 16, 512, 128
NT = S // P
T = B * NT
BANK = 512

RH, RD = 16, 8
HEADS = [(u % 4) * 4 + u // 4 for u in range(RH)]
RCOLS = sum(P * (t + 1) for t in range(NT))
RAT = [BANK, 2 * BANK, BANK + P, 0]

H, DH, W = 8, 64, 64
HP = H // 2
NQ, NKV = 64, 128
ITERS = 50
FETCH = 9.0 / 8.0
UNITS = 2 * NT
HU = H // 2

NP = 32


def host_constants():
    f = np.float32
    c = {}
    c["ident"] = np.eye(P, dtype=f)
    ns = np.zeros((P, 2, 2 * RH), f)
    for p in range(P):
        for o in range(2):
            ns[p, o, RH * o + p % RH] = 1
    c["norm_sel"] = ns.reshape(P, -1)
    c["later_key"] = (np.arange(P)[:, None] > np.arange(P)[None, :]).astype(f)
    c["iota"] = np.concatenate([np.tile(np.arange(NQ + 1, dtype=f), (P, 1)),
                                np.tile(np.arange(NKV, dtype=f), (P, 1))], 1)
    s8 = np.zeros((P, HU, P), f)
    for h in range(HU):
        s8[[h, HU + h], h, :] = -1
    c["spread_unit"] = s8.reshape(P, -1)
    s16 = np.zeros((P, H, P), f)
    for h in range(H):
        s16[[h, H + h], h, :] = -1
    c["spread_all"] = s16.reshape(P, -1)
    rows = np.zeros((P, 4), f)
    k = np.array([NQ] * B + [NKV] * B, np.float64)
    rows[:2 * B, 0] = -np.log(np.minimum(k * FETCH, S).astype(f))
    rows[:2 * B, 1] = k
    rows[:2 * B, 2] = k + 1
    rows[B:2 * B, 3] = 1
    c["router_rows"] = rows
    sg = np.zeros((P, 2), f)
    for g in range(4):
        sg[g * NP:(g + 1) * NP, 0] = (-1, 1, 1, -1)[g]
        sg[g * NP:(g + 1) * NP, 1] = (1, -1, 1, -1)[g]
    c["ssm_sign"] = sg
    return c


def wait(e, sem, v):
    if isinstance(v, int) and v <= 0:
        return
    e.wait_ge(sem, v)


def apart(e):
    e.nop(nofuse=True)


def in_pairs(e, step):
    step(0)
    with e.Fori(1, B // 2 - 1) as i:
        step(i)
    step(B // 2 - 1)


class Semaphores:

    def __init__(self, nc, ctx, prefix):
        self.nc, self.ctx, self.prefix, self.sems = nc, ctx, prefix, []

    def __call__(self, name):
        self.sems.append(self.ctx.enter_context(self.nc.semaphore(self.prefix + name)))
        return self.sems[-1]

    def end(self):
        with self.nc.Block() as block:
            @block.gpsimd
            def _(pool):
                for s in self.sems:
                    pool.sem_clear(s)


class Chain:

    def __init__(self, e, sem):
        self.e, self.sem, self.n = e, sem, 0

    def __call__(self, ins):
        self.n += 1
        ins.then_inc(self.sem, 1)
        self.e.wait_ge(self.sem, self.n)


def stage_load(nc, K, A):
    with ExitStack() as ctx:
        sem = Semaphores(nc, ctx, "ld_")
        xs = [sem(f"x{i}") for i in range(4)]
        ws = sem("w")
        dv = sem("dve")
        st = ctx.enter_context(nc.sbuf_tensor("ld_st", [P, 4, 6], F32))
        work = ctx.enter_context(ExitStack())
        block = work.enter_context(nc.Block())
        x_d = A["x"].rearrange("(t p) d -> p t d", p=P)
        loads = K["loads"]

        @block.sync
        def _(sp):
            for q in range(4):
                n = T // 4
                sp.dma_start(K["x"][:, q * n:(q + 1) * n, :], x_d[:, q * n:(q + 1) * n, :]).then_inc(xs[q], 16)

        @block.scalar
        def _(act):
            for dst, src in loads:
                act.dma_start(dst, src).then_inc(ws, 16)
            act.wait_ge(ws, 16 * len(loads))

        @block.vector
        def _(dve):
            link = Chain(dve, dv)
            dve.wait_ge(ws, 16 * len(loads))
            g = K["gam"]
            link(nc.vector.tensor_scalar(K["negc"][:], g[:], -float(RD) ** -0.5, None, ALU.mult))
            link(nc.vector.tensor_scalar(K["lo"][:], g[:], 0.0, None, ALU.is_lt))
            link(nc.vector.tensor_scalar(K["hi"][:], K["lo"][:], 3e38, 1.0, ALU.mult, ALU.add))
            nc.vector.tensor_copy(K["identb"][:], K["ident"][:])
            nc.vector.tensor_copy(K["spread_unit_b"][:], K["spread_unit"][:])
            link(nc.vector.tensor_copy(K["spread_all_b"][:], K["spread_all"][:]))
            for t in range(T):
                if t % (T // 4) == 0:
                    dve.wait_ge(xs[t // (T // 4)], 16)
                link(nc.vector.bn_stats(st[:, t % 4, :], K["x"][:, t, :]))
                nc.vector.bn_aggr(K["mv"][:, t, :], st[:, t % 4, :])

        work.close()
        sem.end()


def stage_rbf(nc, K):
    with ExitStack() as ctx:
        sb = lambda n, s, d=F32: ctx.enter_context(nc.sbuf_tensor("r_" + n, s, d))
        ps = lambda n, s, d=F32: ctx.enter_context(nc.psum_tensor("r_" + n, s, d))
        sem = Semaphores(nc, ctx, "r_")
        HH = RH // 2
        z = sb("z", [P, NT, P])
        zt = sb("zt", [P, S])
        sq = sb("sq", [P, 2, S])
        part = sb("part", [P, 2, 3, S], BF16)
        rest = sb("rest", [P, 2, S])
        npart = sb("npart", [4 * HH, 3, S], BF16)
        nrest = sb("nrest", [4 * HH, S])
        ops = [sb(n, [P, 2, HH, S], BF16) for n in ("qs", "ks")]
        vp = sb("vp", [P, 2, NT, 4, 160])
        pr = sb("pr", [P, 2, 4, RCOLS])
        ot = sb("ot", [P, S])
        st6 = sb("st6", [P, NT, 6])
        mv4 = sb("mv4", [P, NT, 2])
        rstd = sb("rstd", [P, T])
        dist = ps("dist", [P, 2, 3 * BANK])
        acc = ps("acc", [P, BANK])
        misc = ps("misc", [P, BANK])

        s_sd = sem("std")
        s_ini = sem("ini")
        s_zero = sem("zero")
        s_z = sem("z")
        s_mp = sem("mp")
        s_me = sem("me")
        s_p1 = sem("p1")
        s_sq = sem("sq")
        s_p2 = sem("p2")
        s_p3 = sem("p3")
        s_on = sem("on")
        s_wr = sem("wr")
        s_ld = [sem("ld0"), sem("ld1")]
        s_st = sem("st")
        s_ex = sem("ex")
        s_cl = sem("cl")
        s_mv = sem("mv")
        s_mk = sem("mk")
        s_pv = sem("pv")
        s_ot = sem("ot")
        s_wo = sem("wo")
        s_xa = sem("xa")
        s_bn = sem("bn")
        USES = 5
        AT = (0, 2, 4, 6, 7)
        SLOTS = (((0, 3, 0), (3, 2, 1), (5, 1, 2)),
                 ((0, 1, 0), (1, 1, 1), (2, 1, 2), (3, 1, 0), (4, 1, 1), (5, 1, 0)))
        NORMS = 6 * RD
        ROWS = NORMS + 6
        WRITES = 16 * (sum(len(v) for v in SLOTS) + 2)
        READS = 16 * 4
        rows_d = nc.dram_tensor("rbf_rows", [2, ROWS, 2, HH, S], BF16, kind="Internal").ap()
        work = ctx.enter_context(ExitStack())
        block = work.enter_context(nc.Block())

        heads = HEADS

        @block.sync
        def _(sp):
            sp.wait_ge(s_zero, 2)
            for o in range(2):
                for e in range(2):
                    at = NORMS + 3 * (1 - o)
                    sp.dma_start(rows_d[o, at:at + 3, e], ops[0][0:3, 0]).then_inc(s_on, 16)
            sp.wait_ge(s_on, 16 * 4)

            def batch(b, par, i):
                for o in range(2):
                    sp.wait_ge(s_p3, 3 * b + o + 1)
                    apart(sp)
                    for slot, n, which in SLOTS[o]:
                        src = part[:, o, which, :].unsqueeze(1)
                        if n > 1:
                            src = src.broadcast_to([P, n, S])
                        sp.dma_start(rows_d[o, RD * slot:RD * (slot + n)]
                                     .rearrange("(k d) e h s -> (d e h) k s", d=RD), src).then_inc(s_wr, 16)
                sp.wait_ge(s_p3, 3 * b + 3)
                apart(sp)
                for o in range(2):
                    at = NORMS + 3 * o
                    sp.dma_start(rows_d[o, at:at + 3].rearrange("k e h s -> (e h) k s"),
                                 npart[RH * o:RH * (o + 1)]).then_inc(s_wr, 16)
                sp.wait_ge(s_wr, WRITES * (b + 1))
                apart(sp)
                wait(sp, s_st, RH * (b - 1))
                apart(sp)
                for e in range(2):
                    for o in range(2):
                        sp.dma_start(ops[o][64 * e:64 * e + ROWS, par], rows_d[o, :, e]).then_inc(s_ld[par], 16)
                sp.wait_ge(s_ld[par], READS * (i + 1))
                apart(sp)

            in_pairs(sp, lambda i: [batch(2 * i + e, e, i) for e in range(2)])

        @block.tensor
        def _(pe):
            def use(b, par, k):
                wait(pe, s_me, USES * b + k)
                if k == 0:
                    pe.wait_ge(s_z, b + 1)
                    for j in range(NT):
                        mm = nc.tensor.transpose(misc[:, j * P:(j + 1) * P], z[:, j, :], K["ident"][:])
                elif k < 3:
                    mm = nc.tensor.matmul(misc[:], K[("wq", "wk")[k - 1]][:], zt[:], start=True, stop=True)
                elif k == 3:
                    pe.wait_ge(s_sq, 2 * b + 2)
                    for o in range(2):
                        mm = nc.tensor.matmul(misc[0:4 * HH, :], K["norm_sel"][:, o * 4 * HH:(o + 1) * 4 * HH],
                                              sq[:, o, :], start=o == 0, stop=o == 1)
                else:
                    for j in range(NT):
                        mm = nc.tensor.matmul(misc[:, j * P:(j + 1) * P], zt[:, j * P:(j + 1) * P], K["wv"][:],
                                              start=True, stop=True)
                mm.then_inc(s_mp, 1)

            def scores(b, par, u, i):
                n = RH * b + u
                if u == 0:
                    pe.wait_ge(s_ld[par], READS * (i + 1))
                wait(pe, s_ex, n - 1)
                rows = slice(64 * (u % 2), 64 * (u % 2) + ROWS)
                for t in (3, 0, 2, 1):
                    mm = nc.tensor.matmul(dist[:, u % 2, RAT[t]:RAT[t] + P * (t + 1)],
                                          ops[1][rows, par, u // 2, t * P:(t + 1) * P],
                                          ops[0][rows, par, u // 2, 0:P * (t + 1)], start=True, stop=True)
                mm.then_inc(s_st, 1)

            def values(b, par, q, tiles):
                if tiles[0] == 3:
                    pe.wait_ge(s_mk, RH * b + 4 * q + 4)
                    pe.wait_ge(s_mv, RH * b + 4 * q + 4)
                    if q == 0:
                        pe.wait_ge(s_me, USES * (b + 1))
                        wait(pe, s_ot, b)
                for t in tiles:
                    for g in range(4):
                        mm = nc.tensor.matmul(acc[32 * g:32 * g + 32, 0:P * (t + 1)],
                                              vp[:, par, t, g, 32 * q:32 * q + 32],
                                              pr[:, q % 2, g, RAT[t]:RAT[t] + P * (t + 1)],
                                              start=(q == 0 and t == 3), stop=(q == 3 and t == 0),
                                              skip_group_check=True)
                if tiles[-1] == 0:
                    mm.then_inc(s_pv, 1)

            def output(b, done):
                pe.wait_ge(s_ot, b + 1)
                wait(pe, s_me, done)
                for j in range(NT):
                    mm = nc.tensor.matmul(misc[:, j * P:(j + 1) * P], ot[:, j * P:(j + 1) * P], K["wo"][:],
                                          start=True, stop=True)
                mm.then_inc(s_wo, 1)

            for k in range(USES):
                use(0, 0, k)

            def batch(b, par, i):
                first = isinstance(b, int) and b == 0
                last = isinstance(b, int) and b == B - 1
                for u in range(RH):
                    scores(b, par, u, i)
                    for at, tiles in ((2, (3,)), (3, (2, 1, 0))):
                        if u == at and not first:
                            values(b - 1, 1 - par, 3, tiles)
                        elif u % 4 == at and u > 4:
                            values(b, par, u // 4 - 1, tiles)
                    if u == 9 and not first:
                        output(b - 1, USES * min(b + 2, B) if last else USES * (b + 2))
                    if u in AT and not last:
                        if u == AT[0]:
                            wait(pe, s_xa, b - 1)
                        use(b + 1, 1 - par, AT.index(u))

            in_pairs(pe, lambda i: [batch(2 * i + e, e, i) for e in range(2)])
            values(B - 1, 1, 3, (3, 2, 1, 0))
            output(B - 1, USES * B)

        @block.scalar
        def _(act):
            act.wait_ge(s_ini, 1)
            nc.scalar.activation(rstd[:], rstd[:], ACT.Sqrt).then_inc(s_sd, 1)

            def squares(b, o):
                act.wait_ge(s_mp, USES * b + 2 + o)
                nc.scalar.activation(sq[:, o, :], misc[:], ACT.Square).then_inc(s_sq, 1)

            squares(0, 0)
            squares(0, 1)

            def batch(b, par):
                last = isinstance(b, int) and b == B - 1
                for u in range(RH):
                    n = RH * b + u
                    h = heads[u]
                    act.wait_ge(s_st, n + 1)
                    wait(act, s_pv, 4 * b + u // 4 - 1)
                    nc.scalar.activation(pr[:, u // 4 % 2, u % 4, :], dist[:, u % 2, 0:RCOLS], ACT.Exp,
                                         scale=K["negc"][:, h:h + 1]).then_inc(s_ex, 1)
                    if u in AT[1:3] and not last:
                        squares(b + 1, AT.index(u) - 1)

            in_pairs(act, lambda i: [batch(2 * i + e, e) for e in range(2)])

        @block.vector
        def _(dve):
            nc.vector.tensor_scalar(rstd[:], K["mv"][:, :, 1], 1e-5, None, ALU.add).then_inc(s_ini, 1)
            dve.wait_ge(s_sd, 1)
            nc.vector.reciprocal(rstd[:], rstd[:]).then_inc(s_ini, 1)
            dve.wait_ge(s_ini, 2)

            def norm(b):
                wait(dve, s_mp, USES * (b - 1) + 1)
                for j in range(NT):
                    t = b * NT + j
                    ins = nc.vector.tensor_scalar(z[:, j, :], K["x"][:, t, :], K["mv"][:, t, 0:1],
                                                  rstd[:, bass.ds(t, 1)], ALU.subtract, ALU.mult)
                ins.then_inc(s_z, 1)

            def split(b, src, first, second, rest, scale, n):
                nc.vector.tensor_scalar(first, src, scale, None, ALU.mult).then_inc(s_p1, 1)
                dve.wait_ge(s_p1, 3 * b + n)
                nc.vector.scalar_tensor_tensor(rest, src, scale, first, ALU.mult, ALU.subtract).then_inc(s_me, 1)
                dve.wait_ge(s_me, USES * b + n + 1)
                nc.vector.tensor_copy(second, rest).then_inc(s_p2, 1)

            def leave(b, par, k):
                dve.wait_ge(s_mp, USES * b + k + 1)
                if k == 0:
                    nc.vector.tensor_copy(zt[:], misc[:]).then_inc(s_me, 1)
                elif k < 3:
                    o = k - 1
                    dve.wait_ge(s_sq, 2 * b + k)
                    wait(dve, s_p3, 3 * (b - 1) + k)
                    if o == 0:
                        wait(dve, s_wr, WRITES * b)
                    split(b, misc[:], part[:, o, 0, :], part[:, o, 1, :], rest[:, o, :], (-2.0, 1.0)[o], k)
                elif k == 3:
                    wait(dve, s_p3, 3 * b)
                    split(b, misc[0:4 * HH, :], npart[:, 0, :], npart[:, 1, :], nrest[:], 1.0, k)
                else:
                    if isinstance(b, int) and b == 0:
                        dve.wait_ge(s_zero, 1)
                    nc.vector.tensor_copy(vp[:, par].rearrange("p j g (q c) -> p j g q c", q=4)[:, :, :, :, 0:RD],
                                          misc[:].rearrange("p (j g q d) -> p j g q d", j=NT, g=4, q=4)
                                          ).then_inc(s_me, 1)

            def leave_values(b):
                dve.wait_ge(s_pv, 4 * (b + 1))
                wait(dve, s_wo, b)
                nc.vector.tensor_copy(ot[:], acc[:]).then_inc(s_ot, 1)

            def residual(b):
                dve.wait_ge(s_wo, b + 1)
                xb = K["x"][:, bass.ds(b * NT, NT), :]
                nc.vector.tensor_tensor(xb, xb, misc[:].rearrange("p (j d) -> p j d", j=NT), ALU.add).then_inc(s_xa, 1)
                dve.wait_ge(s_xa, b + 1)
                apart(dve)
                for j in range(NT):
                    ins = nc.vector.bn_stats(st6[:, j, :], K["x"][:, b * NT + j, :])
                ins.then_inc(s_bn, 1)
                dve.wait_ge(s_bn, 3 * b + 1)
                apart(dve)
                for j in range(NT):
                    ins = nc.vector.bn_aggr(mv4[:, j, :], st6[:, j, :])
                ins.then_inc(s_bn, 1)
                dve.wait_ge(s_bn, 3 * b + 2)
                nc.vector.tensor_copy(K["mv"][:, bass.ds(b * NT, NT), :], mv4[:]).then_inc(s_bn, 1)

            def batch(b, par):
                first = isinstance(b, int) and b == 0
                last = isinstance(b, int) and b == B - 1
                for u in range(RH):
                    n = RH * b + u
                    if u == 14 and not (isinstance(b, int) and b >= B - 2):
                        norm(b + 2)
                    dve.wait_ge(s_ex, n + 1)
                    nc.vector.tensor_scalar(pr[:, u // 4 % 2, u % 4, :], pr[:, u // 4 % 2, u % 4, :],
                                            K["hi"][:, heads[u]:heads[u] + 1], K["lo"][:, heads[u]:heads[u] + 1],
                                            ALU.min, ALU.max).then_inc(s_cl, 1)
                    dve.wait_ge(s_cl, n + 1)
                    one = pr[:, u // 4 % 2, u % 4, BANK - P:BANK + P].rearrange("p (k c) -> p k c", k=2)
                    nc.vector.tensor_tensor(one, one, K["later_key"][:].unsqueeze(1).broadcast_to([P, 2, P]),
                                            ALU.mult).then_inc(s_mv, 1)
                    if u == 3 and not first:
                        leave_values(b - 1)
                    if u == 9 and not first:
                        residual(b - 1)
                    if u in AT and not last:
                        leave(b + 1, 1 - par, AT.index(u))

            norm(0)
            for k in range(USES):
                leave(0, 0, k)
            norm(1)
            in_pairs(dve, lambda i: [batch(2 * i + e, e) for e in range(2)])
            leave_values(B - 1)
            residual(B - 1)

        @block.gpsimd
        def _(pool):
            nc.gpsimd.memset(vp[:], 0.0).then_inc(s_zero, 1)
            nc.gpsimd.memset(ops[0][:], 1.0)
            nc.gpsimd.memset(ops[1][:], 1.0).then_inc(s_zero, 1)

            def split(b, k):
                pool.wait_ge(s_p2, 3 * b + k + 1)
                p, r = (part[:, k], rest[:, k, :]) if k < 2 else (npart[:], nrest[:])
                nc.gpsimd.tensor_tensor(p[:, 2, :], r, p[:, 1, :], ALU.subtract).then_inc(s_p3, 1)

            for k in range(3):
                split(0, k)

            def batch(b, par):
                last = isinstance(b, int) and b == B - 1
                for u in range(RH):
                    pool.wait_ge(s_cl, RH * b + u + 1)
                    buf = pr[:, u // 4 % 2, u % 4, :]
                    two = buf[:, RCOLS - 4 * P:RCOLS].rearrange("p (k c) -> p k c", k=2)[:, :, P:2 * P]
                    later = K["later_key"][:].unsqueeze(1).broadcast_to([P, 2, P])
                    nc.gpsimd.tensor_tensor(two, two, later, ALU.mult).then_inc(s_mk, 1)
                    if u in AT[1:4] and not last:
                        split(b + 1, AT.index(u) - 1)

            in_pairs(pool, lambda i: [batch(2 * i + e, e) for e in range(2)])

        work.close()
        sem.end()


def stage_scores(nc, K, tag):
    with ExitStack() as ctx:
        sb = lambda n, s, d=F32: ctx.enter_context(nc.sbuf_tensor(tag + "s_" + n, s, d))
        ps = lambda n, s, d=F32: ctx.enter_context(nc.psum_tensor(tag + "s_" + n, s, d))
        sem = Semaphores(nc, ctx, tag + "s_")
        yb = sb("yb", [P, 2, NT, P])
        yt = sb("yt", [P, 2, S])
        sc = sb("sc", [P, NT, 2, B])
        vy = sb("vy", [P, T])
        two = sb("two", [P, 2, T])
        tp = ps("tp", [P, 2, BANK])
        sp_ = ps("sp", [P, 2, BANK])
        rows = ps("rows", [P, BANK])
        s_d = sem("d")
        s_a = sem("a")
        s_y = sem("y")
        s_yc = sem("yc")
        s_t = sem("t")
        s_te = sem("te")
        s_s = sem("s")
        s_se = sem("se")
        s_r = sem("r")
        s_re = sem("re")
        s_k = sem("k")
        s_l = sem("l")
        work = ctx.enter_context(ExitStack())
        block = work.enter_context(nc.Block())

        @block.vector
        def _(dve):
            link = Chain(dve, s_d)
            link(nc.vector.tensor_scalar(K["rstd"][:], K["mv"][:, :, 1], 1e-5, None, ALU.add))
            dve.wait_ge(s_a, 1)
            link(nc.vector.reciprocal(K["rstd"][:], K["rstd"][:]))
            link(nc.vector.tensor_tensor(vy[:], K["mv"][:, :, 1], K["rstd"][:], ALU.mult))
            link(nc.vector.tensor_tensor(vy[:], vy[:], K["rstd"][:], ALU.mult))
            link(nc.vector.tensor_scalar(two[:, 0, :], vy[:], 1e-5, None, ALU.add))
            link(nc.vector.tensor_scalar(two[:, 1, :], vy[:], float(E), None, ALU.mult))
            dve.wait_ge(s_a, 2)
            link(nc.vector.reciprocal(K["r2"][:], two[:, 0, :]))
            link(nc.vector.tensor_scalar(two[:, 1, :], two[:, 1, :], 1e-12, None, ALU.max))
            link(nc.vector.reciprocal(two[:, 1, :], two[:, 1, :]))
            link(nc.vector.tensor_scalar(K["rc"][:], two[:, 1, :], float(np.sqrt(np.float32(E))), None, ALU.mult))

            def batch(b, par):
                wait(dve, s_yc, b - 1)
                wait(dve, s_t, b - 1)
                for j in range(NT):
                    t = b * NT + j
                    ins = nc.vector.tensor_scalar(yb[:, par, j, :], K["x"][:, t, :], K["mv"][:, t, 0:1],
                                                  K["rstd"][:, bass.ds(t, 1)], ALU.subtract, ALU.mult)
                ins.then_inc(s_y, 1)

            in_pairs(dve, lambda i: [batch(2 * i + e, e) for e in range(2)])
            R = K["router_rows"]
            link(nc.vector.tensor_scalar(K["na"][:], R[0:2 * B, 0:1], float(np.log(np.float32(S))), None, ALU.add))
            dve.wait_ge(s_re, 1)
            link(nc.vector.tensor_reduce(K["smax"][:], K["srow"][:], AX, ALU.max))
            link(nc.vector.tensor_tensor(K["m"][:], K["smax"][:], K["na"][:], ALU.min))
            nc.vector.tensor_scalar(K["shift"][:], K["srow"][:], K["na"][:, 0:1], K["m"][:, 0:1],
                                    ALU.min, ALU.subtract).then_inc(s_k, 1)
            dve.wait_ge(s_l, 2)
            nc.vector.scalar_tensor_tensor(K["na"][:], K["lns"][:], K["m"][:, 0:1], R[0:2 * B, 0:1],
                                           ALU.add, ALU.add)

        @block.scalar
        def _(act):
            act.wait_ge(s_d, 1)
            nc.scalar.activation(K["rstd"][:], K["rstd"][:], ACT.Sqrt).then_inc(s_a, 1)
            act.wait_ge(s_d, 6)
            nc.scalar.activation(two[:], two[:], ACT.Sqrt).then_inc(s_a, 1)

            def batch(b, par):
                act.wait_ge(s_t, b + 1)
                wait(act, s_s, b - 1)
                nc.scalar.activation(yt[:, par, :], tp[:, par, :], ACT.Copy).then_inc(s_te, 1)

                act.wait_ge(s_s, b + 1)
                nc.scalar.activation(sc[:, :, :, bass.ds(b, 1)],
                                     sp_[:, par, 0:2 * NT].rearrange("p (j r o) -> p j r o", j=NT, o=1),
                                     ACT.Copy).then_inc(s_se, 1)

            in_pairs(act, lambda i: [batch(2 * i + e, e) for e in range(2)])
            act.wait_ge(s_r, 1)
            nc.scalar.activation(K["srow"][:], rows[0:2 * B, :], ACT.Copy).then_inc(s_re, 1)
            act.wait_ge(s_k, 1)
            nc.scalar.activation(K["shift"][:], K["shift"][:], ACT.Exp, accum_out=K["sum"][:]).then_inc(s_l, 1)
            act.wait_ge(s_l, 1)
            nc.scalar.activation(K["lns"][:], K["sum"][:], ACT.Ln).then_inc(s_l, 1)

        @block.gpsimd
        def _(pool):
            def batch(b, par):
                pool.wait_ge(s_y, b + 1)
                nc.gpsimd.tensor_copy(K["y"][:, bass.ds(b * NT, NT), :], yb[:, par]).then_inc(s_yc, 1)

            in_pairs(pool, lambda i: [batch(2 * i + e, e) for e in range(2)])

        @block.tensor
        def _(pe):
            def turn(b, par):
                pe.wait_ge(s_y, b + 1)
                wait(pe, s_te, b - 1)
                for j in range(NT):
                    mm = nc.tensor.transpose(tp[:, par, j * P:(j + 1) * P], yb[:, par, j, :], K["ident"][:])
                mm.then_inc(s_t, 1)

            def score(b, par):
                pe.wait_ge(s_te, b + 1)
                wait(pe, s_se, b - 1)
                for j in range(NT):
                    mm = nc.tensor.matmul(sp_[:, par, 2 * j:2 * j + 2], yt[:, par, j * P:(j + 1) * P], K["rt"][:],
                                          start=True, stop=True)
                mm.then_inc(s_s, 1)

            in_pairs(pe, lambda i: [turn(2 * i, 0), turn(2 * i + 1, 1), score(2 * i, 0), score(2 * i + 1, 1)])
            pe.wait_ge(s_se, B)
            for j in range(NT):
                mm = nc.tensor.transpose(rows[0:2 * B, j * P:(j + 1) * P], sc[:, j].rearrange("p r b -> p (r b)"),
                                         K["ident"][:])
            mm.then_inc(s_r, 1)

        work.close()
        sem.end()


def stage_light(nc, K, tag):
    with ExitStack() as ctx:
        sb = lambda n, s, d=F32: ctx.enter_context(nc.sbuf_tensor(tag + "l_" + n, s, d))
        ps = lambda n, s, d=F32: ctx.enter_context(nc.psum_tensor(tag + "l_" + n, s, d))
        sem = Semaphores(nc, ctx, tag + "l_")
        z = sb("z", [P, NT, P])
        xt = sb("xt", [P, S])
        qp = sb("qp", [P, 2, H, S])
        kt = sb("kt", [P, 2, HP, S])
        vv = sb("vv", [P, 2, NT, H, DH + 1])
        mx = sb("mx", [P, HU])
        mh = sb("mh", [P, 2 * HU], BF16)
        mt = sb("mt", [2 * HU, 2, P], BF16)
        pr = sb("pr", [P, 2, HU * (P + W)])
        rden = sb("rden", [P, HU])
        o = sb("o", [P, 2, HU, DH])
        ot = sb("ot", [P, 2, HP, P])
        sm = ps("sm", [P, 2, BANK])
        st = ps("st", [P, 2 * BANK])
        op = ps("op", [P, BANK])
        tb = ps("tb", [P, BANK])
        xb = ps("xb", [P, BANK])
        pj = ps("pj", [P, BANK])

        s_i = sem("i")
        s_z = sem("z")
        s_pp = sem("pp")
        s_pe = sem("pe")
        s_sm = sem("sm")
        s_mx = sem("mx")
        s_t = sem("t")
        s_te = sem("te")
        s_st = sem("st")
        s_ex = sem("ex")
        s_pv = sem("pv")
        s_nm = sem("nm")
        s_ot = sem("ot")
        s_oe = sem("oe")
        s_w = sem("w")
        s_la = sem("la")
        s_sc = sem("sc")
        s_sk = sem("sk")
        s_sl = sem("sl")
        USES = 1 + 2 * HP + NT
        RSTEPS = (1, 3, 5)
        work = ctx.enter_context(ExitStack())
        block = work.enter_context(nc.Block())

        def near(b, par, u, k):
            v = u + k
            if v < 0:
                return b - 1, 1 - par, v + UNITS
            if v >= UNITS:
                return b + 1, 1 - par, v - UNITS
            return b, par, v

        def exists(b, u, k):
            return not (isinstance(b, int) and (b * UNITS + u + k < 0 or b * UNITS + u + k >= B * UNITS))

        @block.tensor
        def _(pe):
            def use(b, par, k):
                wait(pe, s_pe, USES * b + k)
                if k == 0:
                    pe.wait_ge(s_z, b + 1)
                    for j in range(NT):
                        mm = nc.tensor.transpose(pj[:, j * P:(j + 1) * P], z[:, j, :], K["ident"][:])
                elif k <= 2 * HP:
                    mm = nc.tensor.matmul(pj[:], K["wqkv"][:, (k - 1) * P:k * P], xt[:], start=True, stop=True)
                else:
                    j = k - 1 - 2 * HP
                    mm = nc.tensor.matmul(pj[:], xt[:, j * P:(j + 1) * P], K["wqkv"][:, 2 * H * DH:3 * H * DH],
                                          start=True, stop=True)
                mm.then_inc(s_pp, 1)

            def row_scores(b, par, u):
                n = UNITS * b + u
                i, g = u // 2, u % 2
                if u == 0:
                    pe.wait_ge(s_pe, USES * b + 1 + 2 * HP)
                wait(pe, s_mx, 3 * (n - 1) + 1)
                for k in range(HU):
                    h = HU * g + k
                    for half in range(2):
                        w = 2 * i + half
                        lo, hi = max(w - 1, 0), min(w + 2, S // W)
                        out = sm[64 * half:64 * half + 64, k // 2, (k % 2) * 3 * W:(k % 2 + 1) * 3 * W]
                        q = qp[:, par, h, w * W:(w + 1) * W]
                        mm = nc.tensor.matmul(out[:, 0:(hi - lo) * W], q, kt[:, par, h // 2, lo * W:hi * W],
                                              start=True, stop=True)
                        if hi - lo == 2:
                            mm = nc.tensor.matmul(out[:, 2 * W:3 * W], q, kt[:, par, h // 2, lo * W:(lo + 1) * W],
                                                  start=True, stop=True)
                mm.then_inc(s_sm, 1)

            def turn_maxima(b, par, u):
                n = UNITS * b + u
                pe.wait_ge(s_mx, 3 * (n + 1))
                wait(pe, s_te, n)
                nc.tensor.transpose(tb[0:2 * HU, 0:P // 2].bitcast(BF16), mh[:], K["identb"][:]).then_inc(s_t, 1)

            def column_scores(b, par, u):
                n = UNITS * b + u
                i, g = u // 2, u % 2
                wait(pe, s_ex, n)
                pe.wait_ge(s_te, n + 1)
                m = mt[:, u % 2, :]
                for cc in range(HU // 2):
                    c = g * HU // 2 + cc
                    heads = slice(2 * c, 2 * c + 2)

                    def region(rows, at, keys, queries, width):
                        nc.tensor.matmul(st[rows, at + 2 * cc * width:at + 2 * (cc + 1) * width]
                                         .rearrange("p (h q) -> p h q", h=2),
                                         kt[:, par, c, keys], qp[:, par, heads, queries], start=True, stop=False)
                        for k in range(2 * cc, 2 * cc + 2):
                            ins = nc.tensor.matmul(st[rows, at + k * width:at + (k + 1) * width],
                                                   K["spread_unit_b"][0:2 * HU, k * P:k * P + rows.stop - rows.start],
                                                   m[:, queries.start - i * P:queries.stop - i * P],
                                                   start=False, stop=k == 2 * cc + 1)
                        return ins

                    mm = region(slice(0, P), 0, slice(i * P, (i + 1) * P), slice(i * P, (i + 1) * P), P)
                    if i < NT - 1:
                        mm = region(slice(0, 64), BANK, slice((i + 1) * P, (i + 1) * P + W),
                                    slice(i * P + W, (i + 1) * P), W)
                    if i > 0:
                        mm = region(slice(64, P), BANK, slice(i * P - W, i * P), slice(i * P, i * P + W), W)
                mm.then_inc(s_st, 1)

            def values(b, par, u):
                n = UNITS * b + u
                i, g = u // 2, u % 2
                if u == 0:
                    pe.wait_ge(s_pe, USES * (b + 1))
                pe.wait_ge(s_ex, n + 1)
                wait(pe, s_nm, 2 * n)
                for k in range(HU):
                    h = HU * g + k
                    cols = slice(k * (DH + 1), (k + 1) * (DH + 1))
                    p = pr[:, u % 2, :]
                    nc.tensor.matmul(op[:, cols], p[:, k * P:(k + 1) * P], vv[:, par, i, h, :],
                                     start=True, stop=False, skip_group_check=True)
                    at = BANK + k * W
                    if i > 0:
                        mm = nc.tensor.matmul(op[0:64, cols], p[64:P, at:at + W], vv[64:P, par, i - 1, h, :],
                                              start=False, stop=True, skip_group_check=True)
                    if i < NT - 1:
                        mm = nc.tensor.matmul(op[64:P, cols], p[0:64, at:at + W], vv[0:64, par, i + 1, h, :],
                                              start=False, stop=True, skip_group_check=True)
                mm.then_inc(s_pv, 1)

            def turn_values(b, par, u, tiles):
                n = UNITS * b + u
                pe.wait_ge(s_nm, 2 * (n + 1))
                wait(pe, s_la, tiles)
                wait(pe, s_oe, n)
                for c in range(HU // 2):
                    mm = nc.tensor.transpose(xb[:, c * P:(c + 1) * P],
                                             o[:, u % 2, 2 * c:2 * c + 2, :].rearrange("p h d -> p (h d)"),
                                             K["ident"][:])
                mm.then_inc(s_ot, 1)

            def output(t, tpar):
                pe.wait_ge(s_oe, 2 * t + 2)
                wait(pe, s_la, t)
                for c in range(HP):
                    mm = nc.tensor.matmul(xb[:, 0:P], ot[:, tpar, c, :], K["wout_l"][:, c * P:(c + 1) * P],
                                          start=(c == 0), stop=(c == HP - 1))
                mm.then_inc(s_w, 1)

            pe.wait_ge(s_i, 2)
            for k in range(USES):
                use(0, 0, k)
            row_scores(0, 0, 0)
            turn_maxima(0, 0, 0)

            def slot(b, par, u):
                last = isinstance(b, int) and b == B - 1
                tile = NT * b + u // 2 - 2
                if exists(b, u, 1):
                    row_scores(*near(b, par, u, 1))
                if u % 2 == 0 and exists(b, u, -4):
                    output(tile, u // 2 % 2)
                if 2 * u < USES and not last:
                    use(b + 1, 1 - par, 2 * u)
                if not (isinstance(b, int) and b >= B):
                    column_scores(b, par, u)
                if 2 * u + 1 < USES and not last:
                    use(b + 1, 1 - par, 2 * u + 1)
                if exists(b, u, -1):
                    values(*near(b, par, u, -1))
                if exists(b, u, -2):
                    turn_values(*near(b, par, u, -2), tile + 1)
                if exists(b, u, 1):
                    turn_maxima(*near(b, par, u, 1))

            in_pairs(pe, lambda i: [slot(2 * i + e, e, u) for e in range(2) for u in range(UNITS)])
            output(T - 2, 0)
            values(B - 1, 1, UNITS - 1)
            turn_values(B - 1, 1, UNITS - 2, T - 1)
            turn_values(B - 1, 1, UNITS - 1, T - 1)
            output(T - 1, 1)

        @block.scalar
        def _(act):
            def leave(b, par, k):
                act.wait_ge(s_pp, USES * b + k + 1)
                if k == 0:
                    ins = nc.scalar.activation(xt[:], pj[:], ACT.Identity, scale=K["ln_w"][:, 0:1],
                                               bias=K["ln_b"][:, 0:1])
                elif k <= HP:
                    c = k - 1
                    nc.scalar.activation(qp[0:64, par, 2 * c, :], pj[0:64, :], ACT.Copy)
                    ins = nc.scalar.activation(qp[64:P, par, 2 * c + 1, :], pj[64:P, :], ACT.Copy)
                elif k <= 2 * HP:
                    ins = nc.scalar.activation(kt[:, par, k - 1 - HP, :], pj[:], ACT.Copy)
                else:
                    ins = nc.scalar.activation(vv[:, par, k - 1 - 2 * HP, :, 0:DH],
                                               pj[:].rearrange("p (h d) -> p h d", h=H), ACT.Copy)
                ins.then_inc(s_pe, 1)

            def exps(b, par, u):
                n = UNITS * b + u
                i = u // 2
                act.wait_ge(s_st, n + 1)
                wait(act, s_pv, n - 1)
                p = pr[:, u % 2, :]
                scale = float(DH) ** -0.5
                if 0 < i < NT - 1:
                    ins = nc.scalar.activation(p, st[:, 0:HU * (P + W)], ACT.Exp, scale=scale)
                else:
                    rows = slice(0, 64) if i == 0 else slice(64, P)
                    nc.scalar.activation(p[:, 0:BANK], st[:, 0:BANK], ACT.Exp, scale=scale)
                    ins = nc.scalar.activation(p[rows, BANK:], st[rows, BANK:BANK + HU * W], ACT.Exp, scale=scale)
                ins.then_inc(s_ex, 1)

            def leave_values(b, par, u):
                n = UNITS * b + u
                act.wait_ge(s_ot, n + 1)
                if u % 2 == 0:
                    wait(act, s_w, NT * b + u // 2 - 1)
                g = u % 2
                nc.scalar.activation(ot[:, u // 2 % 2, g * HU // 2:(g + 1) * HU // 2, :],
                                     xb[:, 0:HU // 2 * P].rearrange("p (c q) -> p c q", q=P),
                                     ACT.Copy).then_inc(s_oe, 1)

            def route(k):
                act.wait_ge(s_sk, k + 1)
                nc.scalar.activation(K["shift"][:], K["shift"][:], ACT.Exp, accum_out=K["sum"][:]).then_inc(s_sl, 1)
                act.wait_ge(s_sl, 2 * k + 1)
                nc.scalar.activation(K["lns"][:], K["sum"][:], ACT.Ln).then_inc(s_sl, 1)

            act.wait_ge(s_i, 2)
            for k in range(USES):
                leave(0, 0, k)

            def slot(b, par, u):
                last = isinstance(b, int) and b == B - 1
                if 2 * u < USES and not last:
                    leave(b + 1, 1 - par, 2 * u)
                exps(b, par, u)
                if 2 * u + 1 < USES and not last:
                    leave(b + 1, 1 - par, 2 * u + 1)
                if exists(b, u, -2):
                    leave_values(*near(b, par, u, -2))
                if u in RSTEPS:
                    route(len(RSTEPS) * b + RSTEPS.index(u))

            in_pairs(act, lambda i: [slot(2 * i + e, e, u) for e in range(2) for u in range(UNITS)])
            leave_values(B - 1, 1, UNITS - 2)
            leave_values(B - 1, 1, UNITS - 1)

        @block.vector
        def _(dve):
            def maxima(b, par, u):
                n = UNITS * b + u
                dve.wait_ge(s_sm, n + 1)
                nc.vector.tensor_reduce(mx[:], sm[:, :, 0:6 * W].rearrange("p a (k c) -> p a k c", k=2), AX,
                                        ALU.max).then_inc(s_mx, 1)
                dve.wait_ge(s_mx, 3 * n + 1)
                wait(dve, s_t, n)
                nc.vector.tensor_copy(mh[:, 0:HU], mx[:]).then_inc(s_mx, 1)
                dve.wait_ge(s_mx, 3 * n + 2)
                nc.vector.tensor_tensor(mh[:, HU:], mx[:], mh[:, 0:HU], ALU.subtract).then_inc(s_mx, 1)

            def leave_maxima(b, par, u):
                n = UNITS * b + u
                dve.wait_ge(s_t, n + 1)
                wait(dve, s_st, n - 1)
                nc.vector.tensor_copy(mt[:, u % 2, :], tb[0:2 * HU, 0:P // 2].bitcast(BF16)).then_inc(s_te, 1)

            def normalise(b, par, u):
                n = UNITS * b + u
                dve.wait_ge(s_pv, n + 1)
                wait(dve, s_ot, n - 1)
                v = op[:, 0:HU * (DH + 1)].rearrange("p (k c) -> p k c", k=HU)
                nc.vector.reciprocal(rden[:].unsqueeze(2), v[:, :, DH:]).then_inc(s_nm, 1)
                dve.wait_ge(s_nm, 2 * n + 1)
                nc.vector.tensor_tensor(o[:, u % 2], v[:, :, 0:DH], rden[:].unsqueeze(2).broadcast_to([P, HU, DH]),
                                        ALU.mult).then_inc(s_nm, 1)

            def residual(t):
                dve.wait_ge(s_w, t + 1)
                nc.vector.tensor_tensor(K["x"][:, t, :], K["x"][:, t, :], xb[:, 0:P], ALU.add).then_inc(s_la, 1)

            def route_shift(k):
                wait(dve, s_sc, 2 * k)
                nc.vector.tensor_tensor(K["m"][:], K["smax"][:], K["na"][:], ALU.min).then_inc(s_sc, 1)
                dve.wait_ge(s_sc, 2 * k + 1)
                nc.vector.tensor_scalar(K["shift"][:], K["srow"][:], K["na"][:, 0:1], K["m"][:, 0:1],
                                        ALU.min, ALU.subtract).then_inc(s_sk, 1)

            def route_step(k):
                dve.wait_ge(s_sl, 2 * k + 2)
                nc.vector.scalar_tensor_tensor(K["na"][:], K["lns"][:], K["m"][:, 0:1],
                                               K["router_rows"][0:2 * B, 0:1], ALU.add, ALU.add).then_inc(s_sc, 1)

            maxima(0, 0, 0)
            leave_maxima(0, 0, 0)

            def slot(b, par, u):
                if exists(b, u, 1):
                    maxima(*near(b, par, u, 1))
                if u % 2 == 0 and exists(b, u, -4):
                    residual(NT * b + u // 2 - 2)
                if exists(b, u, -1):
                    normalise(*near(b, par, u, -1))
                if exists(b, u, 1):
                    leave_maxima(*near(b, par, u, 1))
                if u - 1 in RSTEPS:
                    route_step(len(RSTEPS) * b + RSTEPS.index(u - 1))
                if u in RSTEPS:
                    route_shift(len(RSTEPS) * b + RSTEPS.index(u))

            in_pairs(dve, lambda i: [slot(2 * i + e, e, u) for e in range(2) for u in range(UNITS)])
            residual(T - 2)
            normalise(B - 1, 1, UNITS - 1)
            residual(T - 1)

        @block.gpsimd
        def _(pool):
            nc.gpsimd.memset(qp[:], 0.0).then_inc(s_i, 1)
            nc.gpsimd.memset(vv[:], 1.0).then_inc(s_i, 1)

            def batch(b):
                wait(pool, s_pp, USES * (b - 1) + 1)
                t = bass.ds(b * NT, NT)
                nc.gpsimd.tensor_tensor(z[:], K["y"][:, t, :],
                                        K["r2"][:, t].unsqueeze(2).broadcast_to([P, NT, P]), ALU.mult).then_inc(s_z, 1)

            in_pairs(pool, lambda i: [batch(2 * i + e) for e in range(2)])

        work.close()
        sem.end()


def stage_topk(nc, K, tag):
    with ExitStack() as ctx:
        sb = lambda n, s, d=F32: ctx.enter_context(nc.sbuf_tensor(tag + "k_" + n, s, d))
        sem = Semaphores(nc, ctx, tag + "k_")
        R2 = 2 * B
        w = sb("w", [R2, S])
        m8 = sb("m8", [R2, S])
        one = sb("one", [R2, S])
        top = sb("top", [R2, 8])
        pp = ctx.enter_context(nc.psum_tensor(tag + "k_pp", [P, BANK], F32))
        s_d, s_a, s_p, s_pl = sem("d"), sem("a"), sem("p"), sem("pl")
        work = ctx.enter_context(ExitStack())
        block = work.enter_context(nc.Block())
        R = K["router_rows"]

        @block.vector
        def _(dve):
            link = Chain(dve, s_d)
            link(nc.vector.tensor_scalar(w[:], K["srow"][:], K["na"][:, 0:1], 0.0, ALU.subtract, ALU.min))
            dve.wait_ge(s_a, 1)
            for r in range(NKV // 8):
                link(nc.vector.max(top[:], w[:]))
                link(nc.vector.match_replace(w[:], top[:], w[:], -1.0))
                if r == NQ // 8 - 1:
                    link(nc.vector.tensor_scalar(m8[:], w[:], 0.0, None, ALU.is_lt))
            link(nc.vector.tensor_scalar(w[:], w[:], 0.0, None, ALU.is_lt))
            link(nc.vector.scalar_tensor_tensor(w[:], m8[:], R[0:R2, 3:4], w[:], ALU.max, ALU.min))
            dve.wait_ge(s_pl, 1)
            link(nc.vector.tensor_tensor_scan(m8[:], one[:], w[:], 0.0, ALU.mult, ALU.add))
            link(nc.vector.scalar_tensor_tensor(m8[:], m8[:], R[0:R2, 2:3], w[:], ALU.subtract, ALU.mult))
            link(nc.vector.tensor_scalar(m8[:], m8[:], R[0:R2, 1:2], None, ALU.add))
            dve.wait_ge(s_p, 1)
            nc.vector.tensor_copy(K["place"][:], pp[:, 0:NT * R2].rearrange("p (j r) -> p j r", j=NT))

        @block.scalar
        def _(act):
            act.wait_ge(s_d, 1)
            nc.scalar.activation(w[:], w[:], ACT.Exp).then_inc(s_a, 1)

        @block.gpsimd
        def _(pool):
            nc.gpsimd.memset(one[:], 1.0).then_inc(s_pl, 1)

        @block.tensor
        def _(pe):
            pe.wait_ge(s_d, 1 + 2 * (NKV // 8) + 1 + 5)
            for j in range(NT):
                mm = nc.tensor.transpose(pp[:, j * R2:(j + 1) * R2], m8[:, j * P:(j + 1) * P], K["ident"][0:R2, 0:R2])
            mm.then_inc(s_p, 1)

        work.close()
        sem.end()


def stage_heavy(nc, K, tag, stats):
    with ExitStack() as ctx:
        sb = lambda n, s, d=F32: ctx.enter_context(nc.sbuf_tensor(tag + "h_" + n, s, d))
        sem = Semaphores(nc, ctx, tag + "h_")
        GC = NQ + 1 + NKV
        yb = sb("yb", [P, 2, NT, P])
        g = sb("g", [P, 2, NT, GC])
        gx = sb("gx", [P, 2, GC])
        gt = sb("gt", [NQ + 1, 2, S])
        qp = sb("qp", [P, 2, H, NQ])
        kt = sb("kt", [P, 2, HP, NKV + 1])
        vv = sb("vv", [P, 2, H, DH + 1])
        nv = sb("nv", [1, H, DH + 1])
        mx = sb("mx", [NQ, 2, H])
        mh = sb("mh", [NQ, 2, 2 * H], BF16)
        mt = sb("mt", [2 * H, 2, NQ], BF16)
        pr = sb("pr", [P, 2, H * NQ])
        pn = sb("pn", [1, 2, H * NQ])
        rden = sb("rden", [NQ, 2, H])
        o = sb("o", [NQ, 2, H, DH])
        ot = sb("ot", [P, 2, HP, NQ])
        hv = sb("hv", [NQ + 1, 2, E])
        st6 = sb("st6", [P, 2, NT, 6])
        mv4 = sb("mv4", [P, 2, NT, 2])
        W_ = ctx.enter_context(nc.psum_tensor(tag + "h_ps", [P, 2, 4, BANK], F32))

        s_i = sem("i")
        s_iv = sem("iv")
        s_y = sem("y")
        s_g = sem("g")
        p_g = sem("pg")
        p_t = sem("pt")
        a_x = sem("ax")
        v_t = sem("vt")
        p_q = sem("pq")
        p_k = sem("pk")
        p_v = sem("pv")
        a_q = sem("aq")
        a_k = sem("ak")
        v_v = sem("vv")
        p_r = sem("pr")
        v_m = sem("vm")
        p_m = sem("pm")
        v_mt = sem("vmt")
        p_c = sem("pc")
        a_e = sem("ae")
        p_o = sem("po")
        v_o = sem("vo")
        p_ot = sem("pot")
        a_ot = sem("aot")
        p_h = sem("ph")
        v_h = sem("vh")
        p_x = sem("px")
        v_x = sem("vx")
        v_s = sem("vs")
        work = ctx.enter_context(ExitStack())
        block = work.enter_context(nc.Block())

        def both(step):
            return lambda i: [step(2 * i + e, e) for e in range(2)]

        @block.tensor
        def _(pe):
            def gather(b, e):
                pe.wait_ge(s_y, b + 1)
                pe.wait_ge(s_g, b + 1)
                wait(pe, a_ot, b - 1)
                for j in range(NT):
                    mm = nc.tensor.matmul(W_[:, e, 0, 0:GC], yb[:, e, j, :], g[:, e, j, :],
                                          start=(j == 0), stop=(j == NT - 1))
                mm.then_inc(p_g, 1)
                wait(pe, v_h, b - 1)
                for j in range(NT):
                    mm = nc.tensor.transpose(W_[0:NQ + 1, e, 1, j * P:(j + 1) * P], g[:, e, j, 0:NQ + 1],
                                             K["ident"][:])
                mm.then_inc(p_t, 1)

            def project(b, e):
                pe.wait_ge(a_x, b + 1)
                wait(pe, v_x, b - 1)
                for c in range(HP):
                    mm = nc.tensor.matmul(W_[:, e, 2, c * NQ:(c + 1) * NQ], K["wq_h"][:, c * P:(c + 1) * P],
                                          gx[:, e, 0:NQ], start=True, stop=True)
                mm.then_inc(p_q, 1)
                for c in range(HP):
                    mm = nc.tensor.matmul(W_[:, e, 0, c * P:(c + 1) * P], K["wk_h"][:, c * P:(c + 1) * P],
                                          gx[:, e, NQ + 1:], start=True, stop=True)
                mm.then_inc(p_k, 1)
                nc.tensor.matmul(W_[:, e, 3, :], gx[:, e, NQ + 1:], K["wv_h"][:], start=True, stop=True).then_inc(p_v, 1)

            def row_scores(b, e):
                pe.wait_ge(a_q, b + 1)
                pe.wait_ge(a_k, b + 1)
                pe.wait_ge(v_t, b + 1)
                for h in range(H):
                    at = (h % 3) * (NKV + 1)
                    mm = nc.tensor.matmul(W_[0:NQ, e, h // 3, at:at + NKV + 1], qp[:, e, h, :], kt[:, e, h // 2, :],
                                          start=True, stop=True)
                mm.then_inc(p_r, 1)

            def turn_maxima(b, e):
                pe.wait_ge(v_m, 4 * b + 4)
                pe.wait_ge(v_v, b + 1)
                apart(pe)
                nc.tensor.transpose(W_[0:2 * H, e, 3, 0:NQ // 2].bitcast(BF16), mh[:, e, :],
                                    K["identb"][0:NQ, 0:NQ]).then_inc(p_m, 1)

            def column_scores(b, e):
                pe.wait_ge(v_mt, b + 1)
                for rows, keys, bank in ((P, slice(0, NKV), 0), (1, slice(NKV, NKV + 1), 1)):
                    for c in range(HP):
                        nc.tensor.matmul(W_[0:rows, e, bank, 2 * c * NQ:2 * (c + 1) * NQ]
                                         .rearrange("p (h q) -> p h q", h=2),
                                         kt[:, e, c, keys], qp[:, e, 2 * c:2 * c + 2, :], start=True, stop=False)
                        for h in range(2 * c, 2 * c + 2):
                            mm = nc.tensor.matmul(W_[0:rows, e, bank, h * NQ:(h + 1) * NQ],
                                                  K["spread_all_b"][0:2 * H, h * P:h * P + rows], mt[:, e, :],
                                                  start=False, stop=h == 2 * c + 1)
                mm.then_inc(p_c, 1)

            def values(b, e):
                pe.wait_ge(a_e, b + 1)
                for h in range(H):
                    out = W_[0:NQ, e, 2 + h // 4, (h % 4) * (DH + 1):(h % 4 + 1) * (DH + 1)]
                    nc.tensor.matmul(out, pr[:, e, h * NQ:(h + 1) * NQ], vv[:, e, h, :], start=True, stop=False)
                    mm = nc.tensor.matmul(out, pn[:, e, h * NQ:(h + 1) * NQ], nv[:, h, :], start=False, stop=True)
                mm.then_inc(p_o, 1)

            def turn_values(b, e):
                pe.wait_ge(v_o, 2 * b + 2)
                apart(pe)
                for c in range(HP):
                    mm = nc.tensor.transpose(W_[:, e, 0, c * NQ:(c + 1) * NQ],
                                             o[:, e, 2 * c:2 * c + 2, :].rearrange("p h d -> p (h d)"),
                                             K["ident"][0:NQ, 0:NQ])
                mm.then_inc(p_ot, 1)

            def output(b, e):
                pe.wait_ge(a_ot, b + 1)
                for c in range(HP):
                    mm = nc.tensor.matmul(W_[0:NQ, e, 1, 0:E], ot[:, e, c, :], K["wout_h"][:, c * E:(c + 1) * E],
                                          start=(c == 0), stop=(c == HP - 1))
                mm.then_inc(p_h, 1)

            def scatter(b, e):
                pe.wait_ge(v_h, b + 1)
                for j in range(NT):
                    mm = nc.tensor.matmul(W_[:, e, 2, j * P:(j + 1) * P], gt[:, e, j * P:(j + 1) * P], hv[:, e, :],
                                          start=True, stop=True)
                mm.then_inc(p_x, 1)

            pe.wait_ge(s_i, 2)
            pe.wait_ge(s_iv, 1)
            in_pairs(pe, lambda i: [both(s)(i) for s in (gather, project, row_scores, turn_maxima, column_scores,
                                                         values, turn_values, output, scatter)])

        @block.scalar
        def _(act):
            def tokens(b, e):
                act.wait_ge(p_g, b + 1)
                wait(act, p_v, b - 1)
                nc.scalar.activation(gx[:, e, :], W_[:, e, 0, 0:GC], ACT.Copy,
                                     scale=K["gam_h"][:, 0:1]).then_inc(a_x, 1)

            def queries(b, e):
                act.wait_ge(p_q, b + 1)
                v = W_[:, e, 2, 0:HP * NQ].rearrange("p (c q) -> p c q", c=HP)
                q = qp[:, e].rearrange("p (c o) q -> p c o q", o=2)
                nc.scalar.activation(q[0:64, :, 0, :], v[0:64], ACT.Copy)
                nc.scalar.activation(q[64:P, :, 1, :], v[64:P], ACT.Copy).then_inc(a_q, 1)

            def keys(b, e):
                act.wait_ge(p_k, b + 1)
                nc.scalar.activation(kt[:, e, :, 0:NKV], W_[:, e, 0, :].rearrange("p (c k) -> p c k", c=HP),
                                     ACT.Copy).then_inc(a_k, 1)

            def exps(b, e):
                act.wait_ge(p_c, b + 1)
                scale = float(DH) ** -0.5
                nc.scalar.activation(pr[:, e, :], W_[:, e, 0, :], ACT.Exp, scale=scale)
                nc.scalar.activation(pn[:, e, :], W_[0:1, e, 1, :], ACT.Exp, scale=scale).then_inc(a_e, 1)

            def values(b, e):
                act.wait_ge(p_ot, b + 1)
                nc.scalar.activation(ot[:, e], W_[:, e, 0, 0:HP * NQ].rearrange("p (c q) -> p c q", c=HP),
                                     ACT.Copy).then_inc(a_ot, 1)

            act.wait_ge(s_i, 2)
            act.wait_ge(s_iv, 1)
            in_pairs(act, lambda i: [both(s)(i) for s in (tokens, queries, keys, exps, values)])

        @block.gpsimd
        def _(pool):
            nc.gpsimd.memset(qp[:], 0.0).then_inc(s_i, 1)
            nc.gpsimd.memset(vv[:], 1.0).then_inc(s_i, 1)

            def scaled(b, e):
                wait(pool, p_g, b - 1)
                t = bass.ds(b * NT, NT)
                nc.gpsimd.tensor_tensor(yb[:, e], K["y"][:, t, :], K["rc"][:, t].unsqueeze(2).broadcast_to([P, NT, P]),
                                        ALU.mult).then_inc(s_y, 1)

            in_pairs(pool, both(scaled))

        @block.vector
        def _(dve):
            nc.vector.memset(nv[:], 1.0).then_inc(v_s, 1)
            dve.wait_ge(v_s, 1)
            nc.vector.tensor_copy(nv[:, :, 0:DH], K["null_v"][:].rearrange("p (h d) -> p h d", h=H))
            for e in range(2):
                nc.vector.tensor_copy(kt[:, e, :, NKV:], K["null_k"][:].unsqueeze(2))
                ins = nc.vector.tensor_copy(hv[NQ:NQ + 1, e, :], K["null_q"][:])
            ins.then_inc(s_iv, 1)

            def onehots(b, e):
                wait(dve, p_t, b - 1)
                place = lambda r: K["place"][:, :, bass.ds(r, 1)]
                nc.vector.tensor_tensor(g[:, e, :, 0:NQ + 1],
                                        K["iota"][:, 0:NQ + 1].unsqueeze(1).broadcast_to([P, NT, NQ + 1]),
                                        place(b).broadcast_to([P, NT, NQ + 1]), ALU.is_equal)
                nc.vector.tensor_tensor(g[:, e, :, NQ + 1:],
                                        K["iota"][:, NQ + 1:].unsqueeze(1).broadcast_to([P, NT, NKV]),
                                        place(b + B).broadcast_to([P, NT, NKV]), ALU.is_equal).then_inc(s_g, 1)

            def turned(b, e):
                dve.wait_ge(p_t, b + 1)
                wait(dve, p_x, b - 1)
                nc.vector.tensor_copy(gt[:, e, :], W_[0:NQ + 1, e, 1, :]).then_inc(v_t, 1)

            def values(b, e):
                dve.wait_ge(p_v, b + 1)
                nc.vector.tensor_copy(vv[:, e, :, 0:DH], W_[:, e, 3, :].rearrange("p (h d) -> p h d", h=H)).then_inc(v_v, 1)

            def maxima(b, e):
                dve.wait_ge(p_r, b + 1)
                k = NKV + 1
                nc.vector.tensor_reduce(mx[:, e, 0:6].rearrange("p (a k) -> p a k", a=2),
                                        W_[0:NQ, e, 0:2, 0:3 * k].rearrange("p a (k c) -> p a k c", k=3),
                                        AX, ALU.max).then_inc(v_m, 1)
                nc.vector.tensor_reduce(mx[:, e, 6:8], W_[0:NQ, e, 2, 0:2 * k].rearrange("p (k c) -> p k c", k=2),
                                        AX, ALU.max).then_inc(v_m, 1)
                dve.wait_ge(v_m, 4 * b + 2)
                nc.vector.tensor_copy(mh[:, e, 0:H], mx[:, e, :]).then_inc(v_m, 1)
                dve.wait_ge(v_m, 4 * b + 3)
                nc.vector.tensor_tensor(mh[:, e, H:], mx[:, e, :], mh[:, e, 0:H], ALU.subtract).then_inc(v_m, 1)

            def leave_maxima(b, e):
                dve.wait_ge(p_m, b + 1)
                nc.vector.tensor_copy(mt[:, e, :], W_[0:2 * H, e, 3, 0:NQ // 2].bitcast(BF16)).then_inc(v_mt, 1)

            def normalise(b, e):
                dve.wait_ge(p_o, b + 1)
                v = W_[0:NQ, e, 2:4, 0:4 * (DH + 1)].rearrange("p a (k c) -> p a k c", k=4)
                r = rden[:, e, :].rearrange("p (a k) -> p a k", a=2).unsqueeze(3)
                nc.vector.reciprocal(r, v[:, :, :, DH:]).then_inc(v_o, 1)
                dve.wait_ge(v_o, 2 * b + 1)
                nc.vector.tensor_tensor(o[:, e].rearrange("p (a k) d -> p a k d", a=2), v[:, :, :, 0:DH],
                                        r.broadcast_to([NQ, 2, 4, DH]), ALU.mult).then_inc(v_o, 1)

            def heavy(b, e):
                dve.wait_ge(p_h, b + 1)
                nc.vector.tensor_copy(hv[0:NQ, e, :], W_[0:NQ, e, 1, 0:E]).then_inc(v_h, 1)

            def residual(b, e):
                dve.wait_ge(p_x, b + 1)
                xb = K["x"][:, bass.ds(b * NT, NT), :]
                nc.vector.tensor_tensor(xb, xb, W_[:, e, 2, :].rearrange("p (j d) -> p j d", j=NT), ALU.add).then_inc(v_x, 1)

            def statistics(b, e):
                dve.wait_ge(v_x, b + 1)
                apart(dve)
                for j in range(NT):
                    ins = nc.vector.bn_stats(st6[:, e, j, :], K["x"][:, b * NT + j, :])
                ins.then_inc(v_s, 1)
                dve.wait_ge(v_s, 3 * b + 2)
                apart(dve)
                for j in range(NT):
                    ins = nc.vector.bn_aggr(mv4[:, e, j, :], st6[:, e, j, :])
                ins.then_inc(v_s, 1)
                dve.wait_ge(v_s, 3 * b + 3)
                nc.vector.tensor_copy(K["mv"][:, bass.ds(b * NT, NT), :], mv4[:, e]).then_inc(v_s, 1)

            onehots(0, 0)
            onehots(1, 1)

            def pair(i):
                last = isinstance(i, int) and i == B // 2 - 1
                for s in (turned, values, maxima, leave_maxima):
                    both(s)(i)
                if not last:
                    both(onehots)(i + 1)
                for s in (normalise, heavy, residual) + ((statistics,) if stats else ()):
                    both(s)(i)

            in_pairs(dve, pair)

        work.close()
        sem.end()


def in_fours(e, step):
    both = lambda q: [step(2 * q + k, k) for k in range(2)]
    both(0)
    with e.Fori(1, B // 4 - 1) as q:
        both(q)
    both(B // 4 - 1)


def stage_ssm(nc, K):
    with ExitStack() as ctx:
        sb = lambda n, s, d=F32: ctx.enter_context(nc.sbuf_tensor("s_" + n, s, d))
        ps = lambda n, s, d=F32: ctx.enter_context(nc.psum_tensor("s_" + n, s, d))
        sem = Semaphores(nc, ctx, "s_")
        c = {n: sb("c_" + n, [P, 1]) for n in ("dt", "mag", "th", "n", "sin", "cos", "t", "lr", "li", "den",
                                               "fr", "fi", "ck", "sk", "ck2", "sk2")}
        bb = sb("bb", [P, P])
        bbt = sb("bbt", [P, P])
        cc = sb("cc", [P, S])
        ss = sb("ss", [P, S])
        tmp = sb("tmp", [P, S])
        dec = sb("dec", [P, S])
        g1 = sb("g1", [P, 2, P])
        g2 = sb("g2", [P, 2, P])
        dd = sb("dd", [P, P])
        vy = sb("vy", [P, T])
        r3 = sb("r3", [P, T])
        xn = sb("xn", [P, 2, 2, NT, P])
        un = sb("un", [P, 2, 2, NT, P])
        ut = sb("ut", [P, 2, 2, S])
        t1 = sb("t1", [P, S])
        t2 = sb("t2", [P, S])
        wi = sb("wi", [P, S])
        wo = sb("wo", [P, S])
        v1 = sb("v1", [P, S])
        v2 = sb("v2", [P, S])
        st6 = sb("st6", [P, 2 * NT, 6])
        mv8 = sb("mv8", [P, 2 * NT, 2])
        tp = ps("tp", [P, 2, BANK])
        xx = ps("xx", [P, 2, BANK])
        yy = ps("yy", [P, 2, BANK])

        s_d = sem("d")
        s_a = sem("a")
        s_b = sem("b")
        s_xn = sem("xn")
        s_un = sem("un")
        s_xx = sem("xxn")
        s_t = sem("t")
        s_te = sem("te")
        s_x = sem("x")
        s_r = sem("r")
        s_w = sem("w")
        s_s = sem("s")
        s_y = sem("y")
        s_o = sem("o")
        s_st = sem("st")
        work = ctx.enter_context(ExitStack())
        block = work.enter_context(nc.Block())
        HALF_PI = float(np.float32(np.pi / 2))
        TURN = 2 * np.pi
        T1 = 6.28125
        T2 = float(np.float32(int((TURN - T1) * 2 ** 21) / 2 ** 21))
        T3 = float(np.float32(TURN - T1 - T2))
        ROUND = float(1.5 * 2 ** 23)
        sign = K["ssm_sign"]

        @block.vector
        def _(dve):
            v = nc.vector
            link = Chain(dve, s_d)
            link(v.tensor_scalar(K["rstd"][:], K["mv"][:, :, 1], 1e-5, None, ALU.add))
            dve.wait_ge(s_a, 1)
            link(v.reciprocal(K["rstd"][:], K["rstd"][:]))
            link(v.tensor_tensor(vy[:], K["mv"][:, :, 1], K["rstd"][:], ALU.mult))
            link(v.tensor_tensor(vy[:], vy[:], K["rstd"][:], ALU.mult))
            link(v.tensor_scalar(r3[:], vy[:], 1e-6, None, ALU.add))
            dve.wait_ge(s_a, 2)
            link(v.reciprocal(r3[:], r3[:]))

            def norm(p, par):
                wait(dve, s_un, p - 1)
                wait(dve, s_xx, p - 1)
                for e in range(2):
                    for j in range(NT):
                        t = (2 * p + e) * NT + j
                        ins = v.tensor_scalar(xn[:, par, e, j, :], K["x"][:, t, :], K["mv"][:, t, 0:1],
                                              K["rstd"][:, bass.ds(t, 1)], ALU.subtract, ALU.mult)
                ins.then_inc(s_xn, 1)

            norm(0, 0)
            dve.wait_ge(s_a, 3)
            link(v.tensor_tensor(c["t"][:], K["lam_re"][:], c["dt"][:], ALU.mult))
            link(v.tensor_tensor(c["th"][:], K["lam_im"][:], c["dt"][:], ALU.mult))
            link(v.tensor_scalar(c["n"][:], c["th"][:], float(1 / TURN), ROUND, ALU.mult, ALU.add))
            link(v.tensor_scalar(c["n"][:], c["n"][:], ROUND, None, ALU.subtract))
            for part in (T1, T2, T3):
                link(v.scalar_tensor_tensor(c["th"][:], c["n"][:], -part, c["th"][:], ALU.mult, ALU.add))
            link(v.tensor_scalar(c["n"][:], c["th"][:], HALF_PI, -TURN, ALU.is_gt, ALU.mult))
            link(v.scalar_tensor_tensor(c["n"][:], c["th"][:], HALF_PI, c["n"][:], ALU.add, ALU.add))
            link(v.tensor_scalar(c["th"][:], c["th"][:], 3.1415925, -3.1415925, ALU.min, ALU.max))
            link(v.tensor_scalar(c["n"][:], c["n"][:], 3.1415925, -3.1415925, ALU.min, ALU.max))
            dve.wait_ge(s_a, 6)
            link(v.tensor_scalar(c["lr"][:], c["cos"][:], c["mag"][:, 0:1], -1.0, ALU.mult, ALU.add))
            link(v.tensor_tensor(c["li"][:], c["sin"][:], c["mag"][:], ALU.mult))
            link(v.tensor_tensor(c["den"][:], K["lam_re"][:], K["lam_re"][:], ALU.mult))
            link(v.scalar_tensor_tensor(c["den"][:], K["lam_im"][:], K["lam_im"][:, 0:1], c["den"][:], ALU.mult, ALU.add))
            link(v.reciprocal(c["den"][:], c["den"][:]))
            link(v.tensor_tensor(c["t"][:], c["li"][:], K["lam_im"][:], ALU.mult))
            link(v.scalar_tensor_tensor(c["fr"][:], c["lr"][:], K["lam_re"][:, 0:1], c["t"][:], ALU.mult, ALU.add))
            link(v.tensor_tensor(c["fr"][:], c["fr"][:], c["den"][:], ALU.mult))
            link(v.tensor_tensor(c["t"][:], c["lr"][:], K["lam_im"][:], ALU.mult))
            link(v.scalar_tensor_tensor(c["fi"][:], c["li"][:], K["lam_re"][:, 0:1], c["t"][:], ALU.mult, ALU.subtract))
            link(v.tensor_tensor(c["fi"][:], c["fi"][:], c["den"][:], ALU.mult))
            link(v.tensor_tensor(c["fi"][:], c["fi"][:], sign[:, 0:1], ALU.mult))
            link(v.tensor_scalar(bb[:], K["b_x2"][:], c["fi"][:, 0:1], None, ALU.mult))
            link(v.scalar_tensor_tensor(bb[:], K["b_x1"][:], c["fr"][:, 0:1], bb[:], ALU.mult, ALU.add))
            v.memset(g1[:], 0.0)
            link(v.memset(g2[:], 0.0))
            for e in range(2):
                for k in range(2):
                    r = slice(64 * e + NP * k, 64 * e + NP * (k + 1))
                    v.tensor_scalar(g1[r, e, :], K["c_x1"][r, :], (2.0, -2.0)[k], None, ALU.mult)
                    v.tensor_scalar(g2[r, e, :], K["c_x2"][r, :], (-2.0, 2.0)[k], None, ALU.mult)
            v.tensor_scalar(dd[:], K["ident"][:], K["ssm_d"][:, 0:1], None, ALU.mult)
            v.memset(dec[:], 1.0)
            v.memset(cc[:, 0:1], 1.0)
            v.memset(ss[:, 0:1], 0.0)
            v.tensor_copy(c["ck"][:], c["cos"][:])
            link(v.tensor_copy(c["sk"][:], c["sin"][:]))
            link(v.tensor_scalar(dec[:], dec[:], c["mag"][:, 0:1], None, ALU.mult))
            n = 1
            while n < S:
                ck, sk = c["ck"], c["sk"]
                v.tensor_scalar(tmp[:, 0:n], ss[:, 0:n], sk[:, 0:1], None, ALU.mult)
                link(v.tensor_scalar(tmp[:, n:2 * n], cc[:, 0:n], sk[:, 0:1], None, ALU.mult))
                v.scalar_tensor_tensor(cc[:, n:2 * n], cc[:, 0:n], ck[:, 0:1], tmp[:, 0:n], ALU.mult, ALU.subtract)
                v.scalar_tensor_tensor(ss[:, n:2 * n], ss[:, 0:n], ck[:, 0:1], tmp[:, n:2 * n], ALU.mult, ALU.add)
                v.tensor_tensor(c["ck2"][:], sk[:], sk[:], ALU.mult)
                link(v.tensor_tensor(c["sk2"][:], ck[:], sk[:], ALU.mult))
                v.scalar_tensor_tensor(ck[:], ck[:], ck[:, 0:1], c["ck2"][:], ALU.mult, ALU.subtract)
                link(v.tensor_scalar(sk[:], c["sk2"][:], 2.0, None, ALU.mult))
                n *= 2
            link(v.tensor_scalar(ss[:], ss[:], sign[:, 1:2], None, ALU.mult))
            ready = link.n
            assert ready == 31 + 1 + 2 + 3 * 9 + 1

            def residual(p, par):
                dve.wait_ge(s_y, p + 1)
                dve.wait_ge(s_xx, p + 1)
                xb = K["x"][:, bass.ds(2 * p * NT, 2 * NT), :]
                v.tensor_tensor(xb, xb, yy[:].rearrange("p e (j d) -> p (e j) d", j=NT), ALU.add).then_inc(s_o, 1)
                dve.wait_ge(s_o, p + 1)
                apart(dve)
                for j in range(2 * NT):
                    ins = v.bn_stats(st6[:, j, :], K["x"][:, 2 * p * NT + j, :])
                ins.then_inc(s_st, 1)
                dve.wait_ge(s_st, 3 * p + 1)
                apart(dve)
                for j in range(2 * NT):
                    ins = v.bn_aggr(mv8[:, j, :], st6[:, j, :])
                ins.then_inc(s_st, 1)
                dve.wait_ge(s_st, 3 * p + 2)
                v.tensor_copy(K["mv"][:, bass.ds(2 * p * NT, 2 * NT), :], mv8[:]).then_inc(s_st, 1)

            def step(p, par):
                last = isinstance(p, int) and p == B // 2 - 1
                dve.wait_ge(s_x, p + 1)
                wait(dve, s_w, p)
                v.tensor_tensor(t1[:], xx[:, 0, :], cc[:], ALU.mult)
                v.tensor_tensor(t2[:], xx[:, 1, :], ss[:], ALU.mult).then_inc(s_r, 1)
                if not last:
                    norm(p + 1, 1 - par)
                dve.wait_ge(s_w, p + 1)
                v.tensor_tensor_scan(wo[:], dec[:], wi[:], 0.0, ALU.mult, ALU.add).then_inc(s_s, 1)
                dve.wait_ge(s_s, 2 * p + 1)
                wait(dve, s_y, p)
                v.tensor_tensor(v1[:], wo[:], cc[:], ALU.mult)
                v.tensor_tensor(v2[:], wo[:], ss[:], ALU.mult).then_inc(s_s, 1)
                if not (isinstance(p, int) and p == 0):
                    residual(p - 1, 1 - par)

            in_fours(dve, step)
            residual(B // 2 - 1, 1)

        @block.scalar
        def _(act):
            a = nc.scalar.activation
            act.wait_ge(s_d, 1)
            a(K["rstd"][:], K["rstd"][:], ACT.Sqrt).then_inc(s_a, 1)
            act.wait_ge(s_d, 5)
            a(r3[:], r3[:], ACT.Sqrt).then_inc(s_a, 1)
            a(c["dt"][:], K["log_step"][:], ACT.Exp).then_inc(s_a, 1)
            act.wait_ge(s_d, 8)
            a(c["mag"][:], c["t"][:], ACT.Exp).then_inc(s_a, 1)
            act.wait_ge(s_d, 17)
            a(c["sin"][:], c["th"][:], ACT.Sin).then_inc(s_a, 1)
            a(c["cos"][:], c["n"][:], ACT.Sin).then_inc(s_a, 1)

            def leave(p, par):
                act.wait_ge(s_t, p + 1)
                wait(act, s_y, p - 1)
                a(ut[:, par], tp[:], ACT.Copy, scale=K["norm_w"][:, 0:1]).then_inc(s_te, 1)

            leave(0, 0)
            act.wait_ge(s_b, 1)
            a(bbt[:], xx[:, 0, 0:P], ACT.Copy).then_inc(s_a, 1)
            in_fours(act, lambda p, par: None if isinstance(p, int) and p == B // 2 - 1 else leave(p + 1, 1 - par))

        @block.gpsimd
        def _(pool):
            pool.wait_ge(s_d, 6)

            def scaled(p, par):
                pool.wait_ge(s_xn, p + 1)
                wait(pool, s_t, p - 1)
                t = bass.ds(2 * p * NT, 2 * NT)
                src = xn[:, par].rearrange("p e j d -> p (e j) d")
                nc.gpsimd.tensor_tensor(un[:, par].rearrange("p e j d -> p (e j) d"), src,
                                        r3[:, t].unsqueeze(2).broadcast_to([P, 2 * NT, P]), ALU.mult).then_inc(s_un, 1)
                nc.gpsimd.tensor_tensor(K["x"][:, t, :], K["x"][:, t, :], src, ALU.add).then_inc(s_xx, 1)

            def step(p, par):
                pool.wait_ge(s_r, p + 1)
                wait(pool, s_s, 2 * p - 1)
                nc.gpsimd.tensor_tensor(wi[:], t1[:], t2[:], ALU.add).then_inc(s_w, 1)
                if not (isinstance(p, int) and p == B // 2 - 1):
                    scaled(p + 1, 1 - par)

            scaled(0, 0)
            in_fours(pool, step)

        @block.tensor
        def _(pe):
            def turn(p, par):
                pe.wait_ge(s_un, p + 1)
                wait(pe, s_te, p)
                for e in range(2):
                    for j in range(NT):
                        mm = nc.tensor.transpose(tp[:, e, j * P:(j + 1) * P], un[:, par, e, j, :], K["ident"][:])
                mm.then_inc(s_t, 1)

            def inputs(p, par):
                pe.wait_ge(s_te, p + 1)
                wait(pe, s_r, p)
                for k in range(2):
                    for e in range(2):
                        mm = nc.tensor.matmul(xx[64 * e:64 * e + 64, k, :], bbt[:, 64 * k:64 * k + 64], ut[:, par, e, :],
                                              start=True, stop=True)
                mm.then_inc(s_x, 1)

            def outputs(p, par):
                pe.wait_ge(s_s, 2 * p + 2)
                wait(pe, s_o, p)
                for e in range(2):
                    for j in range(NT):
                        at = slice(j * P, (j + 1) * P)
                        nc.tensor.matmul(yy[:, e, at], v1[:, at], g1[:, e, :], start=True, stop=False)
                        nc.tensor.matmul(yy[:, e, at], v2[:, at], g2[:, e, :], start=False, stop=False)
                        mm = nc.tensor.matmul(yy[:, e, at], ut[:, par, e, at], dd[:], start=False, stop=True)
                mm.then_inc(s_y, 1)

            turn(0, 0)
            pe.wait_ge(s_d, 31)
            nc.tensor.transpose(xx[:, 0, 0:P], bb[:], K["ident"][:]).then_inc(s_b, 1)
            pe.wait_ge(s_a, 7)

            def step(p, par):
                inputs(p, par)
                if not (isinstance(p, int) and p == B // 2 - 1):
                    turn(p + 1, 1 - par)
                outputs(p, par)

            in_fours(pe, step)

        work.close()
        sem.end()


def program(nc, A, out, stages="rbf f1 ssm f2"):
    with ExitStack() as ctx:
        sb = lambda n, s, d=F32: ctx.enter_context(nc.sbuf_tensor("k_" + n, s, d))
        K = {"x": sb("x", [P, T, E]), "mv": sb("mv", [P, T, 2])}
        loads = []

        def load(name, src, shape):
            K[name] = sb(name, shape)
            loads.append((K[name][:], src))

        for n, rows in (("ident", P), ("norm_sel", P), ("later_key", P),
                        ("iota", P), ("spread_unit", P), ("spread_all", P), ("router_rows", P), ("ssm_sign", P)):
            load(n, A["c_" + n], [rows, A["c_" + n].shape[1]])
        for n in ("wq", "wk", "wv", "wo"):
            load(n, A[n], [P, E])
        load("gam", A["gam"].partition_broadcast(P), [P, RH])
        K["loads"] = loads
        load("wqkv", A["wqkv"], [P, 3 * H * DH])
        for n in ("wout_l", "wq_h", "wk_h", "wv_h", "wout_h"):
            load(n, A[n], [P, H * DH])
        load("rt", A["rt"], [P, 2])
        for n in ("ln_w", "ln_b", "gam_h"):
            load(n, A[n], [P, 1])
        load("null_k", A["null_k"], [P, HP])
        load("null_v", A["null_v"], [1, H * DH])
        load("null_q", A["null_q"], [1, E])
        for n in ("lam_re", "lam_im", "log_step", "ssm_d", "norm_w"):
            load(n, A[n], [P, 1])
        for n in ("b_x1", "b_x2", "c_x1", "c_x2"):
            load(n, A[n], [P, E])
        for n in ("rstd", "r2", "rc"):
            K[n] = sb(n, [P, T])
        for n in ("na", "smax", "m", "sum", "lns"):
            K[n] = sb(n, [2 * B, 1])
        for n in ("srow", "shift"):
            K[n] = sb(n, [2 * B, S])
        K["place"] = sb("place", [P, NT, 2 * B])
        for n in ("negc", "lo", "hi"):
            K[n] = sb(n, [P, RH])
        K["identb"] = sb("identb", [P, P], BF16)
        K["spread_unit_b"] = sb("spread_unit_b", [P, HU * P], BF16)
        K["spread_all_b"] = sb("spread_all_b", [P, H * P], BF16)
        stages = stages.split()
        stage_load(nc, K, A)
        if "rbf" in stages:
            stage_rbf(nc, K)
        if "f1" in stages:
            coarse_to_fine(nc, K, "f1", True)
        if "ssm" in stages:
            stage_ssm(nc, K)
        if "f2" in stages:
            coarse_to_fine(nc, K, "f2", False)
        stage_store(nc, K, out)


def coarse_to_fine(nc, K, tag, stats):
    with nc.sbuf_tensor(tag + "_y", [P, T, E], F32) as K["y"]:
        stage_scores(nc, K, tag)
        stage_light(nc, K, tag)
        stage_topk(nc, K, tag)
        stage_heavy(nc, K, tag, stats)


def stage_store(nc, K, out):
    with nc.semaphore("st_out") as so, nc.Block() as block:
        @block.sync
        def _(sp):
            o_d = out.rearrange("(t p) d -> p t d", p=P)
            for q in range(4):
                n = T // 4
                sp.dma_start(o_d[:, q * n:(q + 1) * n, :], K["x"][:, q * n:(q + 1) * n, :]).then_inc(so, 16)
            sp.wait_ge(so, 64)


def lay_out(inp):
    a = {k: np.asarray(v) for k, v in inp.items()}
    r = {}
    r["x"] = a["L0_attn_a_q"].reshape(B * S, E)
    for n in ("Wq", "Wk", "Wv", "Wo"):
        r[n.lower()] = a["L0_attn_a_" + n]
    order = [HEADS[2 * hh + e] * RD + d for d in range(RD) for e in range(2) for hh in range(RH // 2)]
    for n in ("wq", "wk"):
        r[n] = r[n][:, order]
    r["gam"] = a["L0_attn_a_gamma"].reshape(RH)
    def f(n):
        return a["L0_ffn_" + n]

    def chunks(w):
        return w.reshape(-1, P, w.shape[1]).transpose(1, 0, 2).reshape(P, -1)

    r["wqkv"] = f("Wqkv").T
    r["wout_l"] = chunks(f("Wout_l").T)
    r["wq_h"] = f("Wq").T
    kv = f("Wkv").reshape(H, 2, DH, E)
    r["wk_h"] = kv[:, 0].reshape(H * DH, E).T
    r["wv_h"] = kv[:, 1].reshape(H * DH, E).T
    r["wout_h"] = chunks(f("Wout_h").T)
    r["rt"] = np.concatenate([f("rt_q"), f("rt_kv")]).T
    r["ln_w"], r["ln_b"], r["gam_h"] = (f(n).reshape(E, 1) for n in ("ln_w", "ln_b", "gamma"))
    r["null_k"] = f("null_kv")[0].reshape(HP, P).T
    r["null_v"] = f("null_kv")[1].reshape(1, H * DH)
    r["null_q"] = f("null_q").reshape(1, E)
    d = lambda n: a["L0_attn_b_" + n]
    four = lambda *v: np.concatenate(v).reshape(P, -1)
    for n in ("Lambda_re", "Lambda_im", "log_step"):
        r[n.replace("Lambda", "lam")] = four(*[d(n)] * 4)
    r["ssm_d"], r["norm_w"] = d("D").reshape(P, 1), d("norm_weight").reshape(P, 1)
    br, bi, cr, ci = d("B_re"), d("B_im"), d("C_re").T, d("C_im").T
    r["b_x1"], r["b_x2"] = four(br, bi, bi, br), four(bi, br, br, bi)
    r["c_x1"], r["c_x2"] = four(cr, ci, cr, ci), four(ci, cr, ci, cr)
    for k, v in host_constants().items():
        r["c_" + k] = v
    return {k: np.ascontiguousarray(v) for k, v in r.items()}


def kernel(**inputs):
    import concourse.bacc as bacc
    from concourse.bass_utils import run_bass_kernel_spmd

    nc = bacc.Bacc("TRN2", target_bir_lowering=False, num_devices=1)
    arrays = lay_out(inputs)
    aps = {n: nc.dram_tensor(n, v.shape, mybir.dt.from_np(v.dtype), kind="ExternalInput").ap()
           for n, v in arrays.items()}
    out = nc.dram_tensor("out", (B * S, E), F32, kind="ExternalOutput").ap()
    program(nc, aps, out)
    r = run_bass_kernel_spmd(nc, [arrays], core_ids=[0])
    return r.results[0]["out"].reshape(B, S, E)
```

```python
from contextlib import ExitStack

import numpy as np

import concourse.bass as bass
from concourse import mybir

F32 = mybir.dt.float32
BF16 = mybir.dt.bfloat16
ALU = mybir.AluOpType
ACT = mybir.ActivationFunctionType
AX = mybir.AxisListType.X

P = 128
B, S, E = 16, 512, 128
NT = S // P
T = B * NT
BANK = 512

RH, RD = 16, 8
HEADS = [(u % 4) * 4 + u // 4 for u in range(RH)]
RCOLS = sum(P * (t + 1) for t in range(NT))
RAT = [BANK, 2 * BANK, BANK + P, 0]

H, DH, W = 8, 64, 64
HP = H // 2
NQ, NKV = 64, 128
ITERS = 50
FETCH = 9.0 / 8.0
UNITS = 2 * NT
HU = H // 2

NP = 32


def host_constants():
    f = np.float32
    c = {}
    c["ident"] = np.eye(P, dtype=f)
    ns = np.zeros((P, 2, 2 * RH), f)
    for p in range(P):
        for o in range(2):
            ns[p, o, RH * o + p % RH] = 1
    c["norm_sel"] = ns.reshape(P, -1)
    c["later_key"] = (np.arange(P)[:, None] > np.arange(P)[None, :]).astype(f)
    c["iota"] = np.concatenate([np.tile(np.arange(NQ + 1, dtype=f), (P, 1)),
                                np.tile(np.arange(NKV, dtype=f), (P, 1))], 1)
    rows = np.zeros((P, 4), f)
    k = np.array([NQ] * B + [NKV] * B, np.float64)
    rows[:2 * B, 0] = -np.log(np.minimum(k * FETCH, S).astype(f))
    rows[:2 * B, 1] = k
    rows[:2 * B, 2] = k + 1
    rows[B:2 * B, 3] = 1
    c["router_rows"] = rows
    sg = np.zeros((P, 2), f)
    for g in range(4):
        sg[g * NP:(g + 1) * NP, 0] = (-1, 1, 1, -1)[g]
        sg[g * NP:(g + 1) * NP, 1] = (1, -1, 1, -1)[g]
    c["ssm_sign"] = sg
    return c


def wait(e, sem, v):
    if isinstance(v, int) and v <= 0:
        return
    e.wait_ge(sem, v)


def apart(e):
    e.nop(nofuse=True)


def in_pairs(e, step):
    step(0)
    with e.Fori(1, B // 2 - 1) as i:
        step(i)
    step(B // 2 - 1)


def in_fours(e, step):
    both = lambda q: [step(2 * q + k, k) for k in range(2)]
    both(0)
    with e.Fori(1, B // 4 - 1) as q:
        both(q)
    both(B // 4 - 1)


class Semaphores:

    def __init__(self, nc, ctx, prefix):
        self.nc, self.ctx, self.prefix, self.sems = nc, ctx, prefix, []

    def __call__(self, name):
        self.sems.append(self.ctx.enter_context(self.nc.semaphore(self.prefix + name)))
        return self.sems[-1]

    def end(self):
        with self.nc.Block() as block:
            @block.gpsimd
            def _(pool):
                for s in self.sems:
                    pool.sem_clear(s)


class Chain:

    def __init__(self, e, sem):
        self.e, self.sem, self.n = e, sem, 0

    def __call__(self, ins):
        self.n += 1
        ins.then_inc(self.sem, 1)
        self.e.wait_ge(self.sem, self.n)


def stage_rbf(nc, K, A):
    with ExitStack() as ctx:
        sb = lambda n, s, d=F32: ctx.enter_context(nc.sbuf_tensor("r_" + n, s, d))
        ps = lambda n, s, d=F32: ctx.enter_context(nc.psum_tensor("r_" + n, s, d))
        sem = Semaphores(nc, ctx, "r_")
        HH = RH // 2
        z = sb("z", [P, NT, P])
        zt = sb("zt", [P, S])
        sq = sb("sq", [P, 2, S])
        part = sb("part", [P, 2, 3, S], BF16)
        rest = sb("rest", [P, 2, S])
        npart = sb("npart", [4 * HH, 3, S], BF16)
        nrest = sb("nrest", [4 * HH, S])
        ops = [sb(n, [P, 2, HH, S], BF16) for n in ("qs", "ks")]
        vp = sb("vp", [P, 2, NT, 4, 160])
        pr = sb("pr", [P, 2, 4, RCOLS])
        ot = sb("ot", [P, S])
        st6 = sb("st6", [P, NT, 6])
        mv4 = sb("mv4", [P, NT, 2])
        st = sb("st", [P, T, 6])
        rstd = sb("rstd", [P, T])
        dist = ps("dist", [P, 2, 3 * BANK])
        acc = ps("acc", [P, BANK])
        misc = ps("misc", [P, BANK])

        s_x = [sem(f"x{q}") for q in range(4)]
        s_w = sem("w")
        s_late = sem("late")
        s_sd = sem("std")
        s_ini = sem("ini")
        s_zero = sem("zero")
        s_z = sem("z")
        s_mp = sem("mp")
        s_me = sem("me")
        s_p1 = sem("p1")
        s_sq = sem("sq")
        s_p2 = sem("p2")
        s_p3 = sem("p3")
        s_on = sem("on")
        s_wr = sem("wr")
        s_ld = [sem("ld0"), sem("ld1")]
        s_st = sem("st")
        s_ex = sem("ex")
        s_cl = sem("cl")
        s_mv = sem("mv")
        s_mk = sem("mk")
        s_pv = sem("pv")
        s_ot = sem("ot")
        s_wo = sem("wo")
        s_xa = sem("xa")
        s_bn = sem("bn")
        USES = 5
        AT = (0, 2, 4, 6, 9)
        SLOTS = (((0, 3, 0), (3, 2, 1), (5, 1, 2)),
                 ((0, 1, 0), (1, 1, 1), (2, 1, 2), (3, 1, 0), (4, 1, 1), (5, 1, 0)))
        NORMS = 6 * RD
        ROWS = NORMS + 6
        WRITES = 16 * (sum(len(v) for v in SLOTS) + 2)
        READS = 16 * 4
        rows_d = nc.dram_tensor("rbf_rows", [2, ROWS, 2, HH, S], BF16, kind="Internal").ap()
        work = ctx.enter_context(ExitStack())
        block = work.enter_context(nc.Block())

        heads = HEADS
        FIRST, REST = slice(0, T // 4), slice(T // 4, T)

        @block.sync
        def _(sp):
            x_d = A["x"].rearrange("(t p) d -> p t d", p=P)
            for q in range(4):
                t = slice(q * T // 4, (q + 1) * T // 4)
                sp.dma_start(K["x"][:, t, :], x_d[:, t, :]).then_inc(s_x[q], 16)
            for dst, src in K["later"]:
                sp.dma_start(dst, src).then_inc(s_late, 16)
            sp.wait_ge(s_zero, 2)
            for o in range(2):
                for e in range(2):
                    at = NORMS + 3 * (1 - o)
                    sp.dma_start(rows_d[o, at:at + 3, e], ops[0][0:3, 0]).then_inc(s_on, 16)
            sp.wait_ge(s_on, 16 * 4)

            def batch(b, par, i):
                for o in range(2):
                    sp.wait_ge(s_p3, 3 * b + o + 1)
                    apart(sp)
                    for slot, n, which in SLOTS[o]:
                        src = part[:, o, which, :].unsqueeze(1)
                        if n > 1:
                            src = src.broadcast_to([P, n, S])
                        sp.dma_start(rows_d[o, RD * slot:RD * (slot + n)]
                                     .rearrange("(k d) e h s -> (d e h) k s", d=RD), src).then_inc(s_wr, 16)
                sp.wait_ge(s_p3, 3 * b + 3)
                apart(sp)
                for o in range(2):
                    at = NORMS + 3 * o
                    sp.dma_start(rows_d[o, at:at + 3].rearrange("k e h s -> (e h) k s"),
                                 npart[RH * o:RH * (o + 1)]).then_inc(s_wr, 16)
                sp.wait_ge(s_wr, WRITES * (b + 1))
                apart(sp)
                wait(sp, s_st, RH * (b - 1))
                apart(sp)
                for e in range(2):
                    for o in range(2):
                        sp.dma_start(ops[o][64 * e:64 * e + ROWS, par], rows_d[o, :, e]).then_inc(s_ld[par], 16)
                sp.wait_ge(s_ld[par], READS * (i + 1))
                apart(sp)

            in_pairs(sp, lambda i: [batch(2 * i + e, e, i) for e in range(2)])
            sp.wait_ge(s_late, 16 * len(K["later"]))

        @block.tensor
        def _(pe):
            def use(b, par, k):
                wait(pe, s_me, USES * b + k)
                if k == 0:
                    pe.wait_ge(s_z, b + 1)
                    for j in range(NT):
                        mm = nc.tensor.transpose(misc[:, j * P:(j + 1) * P], z[:, j, :], K["ident"][:])
                elif k < 3:
                    mm = nc.tensor.matmul(misc[:], K[("wq", "wk")[k - 1]][:], zt[:], start=True, stop=True)
                elif k == 3:
                    pe.wait_ge(s_sq, 2 * b + 2)
                    for o in range(2):
                        mm = nc.tensor.matmul(misc[0:4 * HH, :], K["norm_sel"][:, o * 4 * HH:(o + 1) * 4 * HH],
                                              sq[:, o, :], start=o == 0, stop=o == 1)
                else:
                    for j in range(NT):
                        mm = nc.tensor.matmul(misc[:, j * P:(j + 1) * P], zt[:, j * P:(j + 1) * P], K["wv"][:],
                                              start=True, stop=True)
                mm.then_inc(s_mp, 1)

            def scores(b, par, u, i):
                n = RH * b + u
                if u == 0:
                    pe.wait_ge(s_ld[par], READS * (i + 1))
                wait(pe, s_ex, n - 1)
                rows = slice(64 * (u % 2), 64 * (u % 2) + ROWS)
                for t in (3, 0, 2, 1):
                    mm = nc.tensor.matmul(dist[:, u % 2, RAT[t]:RAT[t] + P * (t + 1)],
                                          ops[1][rows, par, u // 2, t * P:(t + 1) * P],
                                          ops[0][rows, par, u // 2, 0:P * (t + 1)], start=True, stop=True)
                mm.then_inc(s_st, 1)

            def values(b, par, q, tiles):
                if tiles[0] == 3:
                    pe.wait_ge(s_mk, RH * b + 4 * q + 4)
                    pe.wait_ge(s_mv, RH * b + 4 * q + 4)
                    if q == 0:
                        pe.wait_ge(s_me, USES * (b + 1))
                        wait(pe, s_ot, b)
                for t in tiles:
                    for g in range(4):
                        mm = nc.tensor.matmul(acc[32 * g:32 * g + 32, 0:P * (t + 1)],
                                              vp[:, par, t, g, 32 * q:32 * q + 32],
                                              pr[:, q % 2, g, RAT[t]:RAT[t] + P * (t + 1)],
                                              start=(q == 0 and t == 3), stop=(q == 3 and t == 0),
                                              skip_group_check=True)
                if tiles[-1] == 0:
                    mm.then_inc(s_pv, 1)

            def output(b, done):
                pe.wait_ge(s_ot, b + 1)
                wait(pe, s_me, done)
                for j in range(NT):
                    mm = nc.tensor.matmul(misc[:, j * P:(j + 1) * P], ot[:, j * P:(j + 1) * P], K["wo"][:],
                                          start=True, stop=True)
                mm.then_inc(s_wo, 1)

            pe.wait_ge(s_w, 16 * len(K["first"]))
            for k in range(USES):
                use(0, 0, k)

            def batch(b, par, i):
                first = isinstance(b, int) and b == 0
                last = isinstance(b, int) and b == B - 1
                for u in range(RH):
                    scores(b, par, u, i)
                    for at, tiles in ((2, (3,)), (3, (2, 1, 0))):
                        if u == at and not first:
                            values(b - 1, 1 - par, 3, tiles)
                        elif u % 4 == at and u > 4:
                            values(b, par, u // 4 - 1, tiles)
                    if u == 10 and not first:
                        output(b - 1, USES * min(b + 2, B) if last else USES * (b + 2))
                    if u in AT and not last:
                        if u == AT[0]:
                            wait(pe, s_xa, b - 1)
                        use(b + 1, 1 - par, AT.index(u))

            in_pairs(pe, lambda i: [batch(2 * i + e, e, i) for e in range(2)])
            values(B - 1, 1, 3, (3, 2, 1, 0))
            output(B - 1, USES * B)

        @block.scalar
        def _(act):
            for dst, src in K["first"]:
                act.dma_start(dst, src).then_inc(s_w, 16)

            def roots(tiles, done):
                act.wait_ge(s_ini, done)
                nc.scalar.activation(rstd[:, tiles], rstd[:, tiles], ACT.Sqrt).then_inc(s_sd, 1)

            roots(FIRST, 3)

            def squares(b, o):
                act.wait_ge(s_mp, USES * b + 2 + o)
                nc.scalar.activation(sq[:, o, :], misc[:], ACT.Square).then_inc(s_sq, 1)

            def leave(b, par, k):
                act.wait_ge(s_mp, USES * b + k + 1)
                if k == 0:
                    nc.scalar.activation(zt[:], misc[:], ACT.Copy).then_inc(s_me, 1)
                else:
                    if isinstance(b, int) and b == 0:
                        act.wait_ge(s_zero, 1)
                    nc.scalar.activation(vp[:, par].rearrange("p j g (q c) -> p j g q c", q=4)[:, :, :, :, 0:RD],
                                         misc[:].rearrange("p (j g q d) -> p j g q d", j=NT, g=4, q=4),
                                         ACT.Copy).then_inc(s_me, 1)

            leave(0, 0, 0)
            squares(0, 0)
            squares(0, 1)
            leave(0, 0, 4)
            roots(REST, 7)
            act.wait_ge(s_ini, 11)

            def batch(b, par):
                last = isinstance(b, int) and b == B - 1
                for u in range(RH):
                    n = RH * b + u
                    h = heads[u]
                    act.wait_ge(s_st, n + 1)
                    wait(act, s_pv, 4 * b + u // 4 - 1)
                    nc.scalar.activation(pr[:, u // 4 % 2, u % 4, :], dist[:, u % 2, 0:RCOLS], ACT.Exp,
                                         scale=K["negc"][:, h:h + 1]).then_inc(s_ex, 1)
                    if u in AT[1:3] and not last:
                        squares(b + 1, AT.index(u) - 1)
                    if u in (AT[0], AT[4]) and not last:
                        leave(b + 1, 1 - par, AT.index(u))

            in_pairs(act, lambda i: [batch(2 * i + e, e) for e in range(2)])

        @block.vector
        def _(dve):
            link = Chain(dve, s_ini)

            def scales(tiles, roots_done):
                for t in range(tiles.start, tiles.stop):
                    ins = nc.vector.bn_stats(st[:, t, :], K["x"][:, t, :])
                link(ins)
                for t in range(tiles.start, tiles.stop):
                    ins = nc.vector.bn_aggr(K["mv"][:, t, :], st[:, t, :])
                link(ins)
                link(nc.vector.tensor_scalar(rstd[:, tiles], K["mv"][:, tiles, 1], 1e-5, None, ALU.add))
                dve.wait_ge(s_sd, roots_done)
                link(nc.vector.reciprocal(rstd[:, tiles], rstd[:, tiles]))

            dve.wait_ge(s_x[0], 16)
            scales(FIRST, 1)

            def norm(b):
                wait(dve, s_mp, USES * (b - 1) + 1)
                for j in range(NT):
                    t = b * NT + j
                    ins = nc.vector.tensor_scalar(z[:, j, :], K["x"][:, t, :], K["mv"][:, t, 0:1],
                                                  rstd[:, bass.ds(t, 1)], ALU.subtract, ALU.mult)
                ins.then_inc(s_z, 1)

            def split(b, src, first, second, rest, scale, n):
                nc.vector.tensor_scalar(first, src, scale, None, ALU.mult).then_inc(s_p1, 1)
                dve.wait_ge(s_p1, 3 * b + n)
                nc.vector.scalar_tensor_tensor(rest, src, scale, first, ALU.mult, ALU.subtract).then_inc(s_me, 1)
                dve.wait_ge(s_me, USES * b + n + 1)
                nc.vector.tensor_copy(second, rest).then_inc(s_p2, 1)

            def leave(b, par, k):
                if k in (0, 4):
                    return
                dve.wait_ge(s_mp, USES * b + k + 1)
                if k < 3:
                    o = k - 1
                    dve.wait_ge(s_sq, 2 * b + k)
                    wait(dve, s_p3, 3 * (b - 1) + k)
                    if o == 0:
                        wait(dve, s_wr, WRITES * b)
                    split(b, misc[:], part[:, o, 0, :], part[:, o, 1, :], rest[:, o, :], (-2.0, 1.0)[o], k)
                elif k == 3:
                    wait(dve, s_p3, 3 * b)
                    split(b, misc[0:4 * HH, :], npart[:, 0, :], npart[:, 1, :], nrest[:], 1.0, k)

            def leave_values(b):
                dve.wait_ge(s_pv, 4 * (b + 1))
                wait(dve, s_wo, b)
                nc.vector.tensor_copy(ot[:], acc[:]).then_inc(s_ot, 1)

            def residual(b):
                dve.wait_ge(s_wo, b + 1)
                xb = K["x"][:, bass.ds(b * NT, NT), :]
                nc.vector.tensor_tensor(xb, xb, misc[:].rearrange("p (j d) -> p j d", j=NT), ALU.add).then_inc(s_xa, 1)
                dve.wait_ge(s_xa, b + 1)
                apart(dve)
                for j in range(NT):
                    ins = nc.vector.bn_stats(st6[:, j, :], K["x"][:, b * NT + j, :])
                ins.then_inc(s_bn, 1)
                dve.wait_ge(s_bn, 3 * b + 1)
                apart(dve)
                for j in range(NT):
                    ins = nc.vector.bn_aggr(mv4[:, j, :], st6[:, j, :])
                ins.then_inc(s_bn, 1)
                dve.wait_ge(s_bn, 3 * b + 2)
                nc.vector.tensor_copy(K["mv"][:, bass.ds(b * NT, NT), :], mv4[:]).then_inc(s_bn, 1)

            def batch(b, par):
                first = isinstance(b, int) and b == 0
                last = isinstance(b, int) and b == B - 1
                for u in range(RH):
                    n = RH * b + u
                    if u == 14 and not (isinstance(b, int) and b >= B - 2):
                        norm(b + 2)
                    dve.wait_ge(s_ex, n + 1)
                    nc.vector.tensor_scalar(pr[:, u // 4 % 2, u % 4, :], pr[:, u // 4 % 2, u % 4, :],
                                            K["hi"][:, heads[u]:heads[u] + 1], K["lo"][:, heads[u]:heads[u] + 1],
                                            ALU.min, ALU.max).then_inc(s_cl, 1)
                    dve.wait_ge(s_cl, n + 1)
                    one = pr[:, u // 4 % 2, u % 4, BANK - P:BANK + P].rearrange("p (k c) -> p k c", k=2)
                    nc.vector.tensor_tensor(one, one, K["later_key"][:].unsqueeze(1).broadcast_to([P, 2, P]),
                                            ALU.mult).then_inc(s_mv, 1)
                    if u == 3 and not first:
                        leave_values(b - 1)
                    if u == 10 and not first:
                        residual(b - 1)
                    if u in AT and not last:
                        leave(b + 1, 1 - par, AT.index(u))

            norm(0)
            for k in range(USES):
                leave(0, 0, k)
            for q in range(1, 4):
                dve.wait_ge(s_x[q], 16)
            scales(REST, 2)
            dve.wait_ge(s_w, 16 * len(K["first"]))
            link(nc.vector.tensor_scalar(K["negc"][:], K["gam"][:], -float(RD) ** -0.5, None, ALU.mult))
            link(nc.vector.tensor_scalar(K["lo"][:], K["gam"][:], 0.0, None, ALU.is_lt))
            link(nc.vector.tensor_scalar(K["hi"][:], K["lo"][:], 3e38, 1.0, ALU.mult, ALU.add))
            norm(1)
            in_pairs(dve, lambda i: [batch(2 * i + e, e) for e in range(2)])
            leave_values(B - 1)
            residual(B - 1)

        @block.gpsimd
        def _(pool):
            nc.gpsimd.memset(vp[:], 0.0).then_inc(s_zero, 1)
            nc.gpsimd.memset(ops[0][:], 1.0)
            nc.gpsimd.memset(ops[1][:], 1.0).then_inc(s_zero, 1)

            def split(b, k):
                pool.wait_ge(s_p2, 3 * b + k + 1)
                p, r = (part[:, k], rest[:, k, :]) if k < 2 else (npart[:], nrest[:])
                nc.gpsimd.tensor_tensor(p[:, 2, :], r, p[:, 1, :], ALU.subtract).then_inc(s_p3, 1)

            for k in range(3):
                split(0, k)

            pool.wait_ge(s_w, 16 * len(K["first"]))

            def batch(b, par):
                last = isinstance(b, int) and b == B - 1
                for u in range(RH):
                    pool.wait_ge(s_cl, RH * b + u + 1)
                    buf = pr[:, u // 4 % 2, u % 4, :]
                    two = buf[:, RCOLS - 4 * P:RCOLS].rearrange("p (k c) -> p k c", k=2)[:, :, P:2 * P]
                    later = K["later_key"][:].unsqueeze(1).broadcast_to([P, 2, P])
                    nc.gpsimd.tensor_tensor(two, two, later, ALU.mult).then_inc(s_mk, 1)
                    if u in AT[1:4] and not last:
                        split(b + 1, AT.index(u) - 1)

            in_pairs(pool, lambda i: [batch(2 * i + e, e) for e in range(2)])

        work.close()
        sem.end()


def stage_scores(nc, K, tag):
    with ExitStack() as ctx:
        sb = lambda n, s, d=F32: ctx.enter_context(nc.sbuf_tensor(tag + "s_" + n, s, d))
        ps = lambda n, s, d=F32: ctx.enter_context(nc.psum_tensor(tag + "s_" + n, s, d))
        sem = Semaphores(nc, ctx, tag + "s_")
        yb = sb("yb", [P, 2, NT, P])
        yt = sb("yt", [P, 2, S])
        sc = sb("sc", [P, NT, 2, B])
        vy = sb("vy", [P, T])
        two = sb("two", [P, 2, T])
        tp = ps("tp", [P, 2, BANK])
        sp_ = ps("sp", [P, 2, BANK])
        rows = ps("rows", [P, BANK])
        s_d = sem("d")
        s_a = sem("a")
        s_y = sem("y")
        s_yc = sem("yc")
        s_t = sem("t")
        s_te = sem("te")
        s_s = sem("s")
        s_se = sem("se")
        s_r = sem("r")
        s_re = sem("re")
        s_k = sem("k")
        s_l = sem("l")
        work = ctx.enter_context(ExitStack())
        block = work.enter_context(nc.Block())

        @block.vector
        def _(dve):
            link = Chain(dve, s_d)
            link(nc.vector.tensor_scalar(K["rstd"][:], K["mv"][:, :, 1], 1e-5, None, ALU.add))
            dve.wait_ge(s_a, 1)
            link(nc.vector.reciprocal(K["rstd"][:], K["rstd"][:]))
            link(nc.vector.tensor_tensor(vy[:], K["mv"][:, :, 1], K["rstd"][:], ALU.mult))
            link(nc.vector.tensor_tensor(vy[:], vy[:], K["rstd"][:], ALU.mult))
            link(nc.vector.tensor_scalar(two[:, 0, :], vy[:], 1e-5, None, ALU.add))
            link(nc.vector.tensor_scalar(two[:, 1, :], vy[:], float(E), None, ALU.mult))
            dve.wait_ge(s_a, 2)
            link(nc.vector.reciprocal(K["r2"][:], two[:, 0, :]))
            link(nc.vector.tensor_scalar(two[:, 1, :], two[:, 1, :], 1e-12, None, ALU.max))
            link(nc.vector.reciprocal(two[:, 1, :], two[:, 1, :]))
            link(nc.vector.tensor_scalar(K["rc"][:], two[:, 1, :], float(np.sqrt(np.float32(E))), None, ALU.mult))

            def batch(b, par):
                wait(dve, s_yc, b - 1)
                wait(dve, s_t, b - 1)
                for j in range(NT):
                    t = b * NT + j
                    ins = nc.vector.tensor_scalar(yb[:, par, j, :], K["x"][:, t, :], K["mv"][:, t, 0:1],
                                                  K["rstd"][:, bass.ds(t, 1)], ALU.subtract, ALU.mult)
                ins.then_inc(s_y, 1)

            in_pairs(dve, lambda i: [batch(2 * i + e, e) for e in range(2)])
            R = K["router_rows"]
            link(nc.vector.tensor_scalar(K["na"][:], R[0:2 * B, 0:1], float(np.log(np.float32(S))), None, ALU.add))
            dve.wait_ge(s_re, 1)
            link(nc.vector.tensor_reduce(K["smax"][:], K["srow"][:], AX, ALU.max))
            link(nc.vector.tensor_tensor(K["m"][:], K["smax"][:], K["na"][:], ALU.min))
            nc.vector.tensor_scalar(K["shift"][:], K["srow"][:], K["na"][:, 0:1], K["m"][:, 0:1],
                                    ALU.min, ALU.subtract).then_inc(s_k, 1)
            dve.wait_ge(s_l, 2)
            nc.vector.scalar_tensor_tensor(K["na"][:], K["lns"][:], K["m"][:, 0:1], R[0:2 * B, 0:1],
                                           ALU.add, ALU.add)

        @block.scalar
        def _(act):
            act.wait_ge(s_d, 1)
            nc.scalar.activation(K["rstd"][:], K["rstd"][:], ACT.Sqrt).then_inc(s_a, 1)
            act.wait_ge(s_d, 6)
            nc.scalar.activation(two[:], two[:], ACT.Sqrt).then_inc(s_a, 1)

            def batch(b, par):
                act.wait_ge(s_t, b + 1)
                wait(act, s_s, b - 1)
                nc.scalar.activation(yt[:, par, :], tp[:, par, :], ACT.Copy).then_inc(s_te, 1)

                act.wait_ge(s_s, b + 1)
                nc.scalar.activation(sc[:, :, :, bass.ds(b, 1)],
                                     sp_[:, par, 0:2 * NT].rearrange("p (j r o) -> p j r o", j=NT, o=1),
                                     ACT.Copy).then_inc(s_se, 1)

            in_pairs(act, lambda i: [batch(2 * i + e, e) for e in range(2)])
            act.wait_ge(s_r, 1)
            nc.scalar.activation(K["srow"][:], rows[0:2 * B, :], ACT.Copy).then_inc(s_re, 1)
            act.wait_ge(s_k, 1)
            nc.scalar.activation(K["shift"][:], K["shift"][:], ACT.Exp, accum_out=K["sum"][:]).then_inc(s_l, 1)
            act.wait_ge(s_l, 1)
            nc.scalar.activation(K["lns"][:], K["sum"][:], ACT.Ln).then_inc(s_l, 1)

        @block.gpsimd
        def _(pool):
            def batch(b, par):
                pool.wait_ge(s_y, b + 1)
                nc.gpsimd.tensor_copy(K["y"][:, bass.ds(b * NT, NT), :], yb[:, par]).then_inc(s_yc, 1)

            in_pairs(pool, lambda i: [batch(2 * i + e, e) for e in range(2)])

        @block.tensor
        def _(pe):
            def turn(b, par):
                pe.wait_ge(s_y, b + 1)
                wait(pe, s_te, b - 1)
                for j in range(NT):
                    mm = nc.tensor.transpose(tp[:, par, j * P:(j + 1) * P], yb[:, par, j, :], K["ident"][:])
                mm.then_inc(s_t, 1)

            def score(b, par):
                pe.wait_ge(s_te, b + 1)
                wait(pe, s_se, b - 1)
                for j in range(NT):
                    mm = nc.tensor.matmul(sp_[:, par, 2 * j:2 * j + 2], yt[:, par, j * P:(j + 1) * P], K["rt"][:],
                                          start=True, stop=True)
                mm.then_inc(s_s, 1)

            in_pairs(pe, lambda i: [turn(2 * i, 0), turn(2 * i + 1, 1), score(2 * i, 0), score(2 * i + 1, 1)])
            pe.wait_ge(s_se, B)
            for j in range(NT):
                mm = nc.tensor.transpose(rows[0:2 * B, j * P:(j + 1) * P], sc[:, j].rearrange("p r b -> p (r b)"),
                                         K["ident"][:])
            mm.then_inc(s_r, 1)

        work.close()
        sem.end()


def stage_light(nc, K, tag):
    with ExitStack() as ctx:
        sb = lambda n, s, d=F32: ctx.enter_context(nc.sbuf_tensor(tag + "l_" + n, s, d))
        ps = lambda n, s, d=F32: ctx.enter_context(nc.psum_tensor(tag + "l_" + n, s, d))
        sem = Semaphores(nc, ctx, tag + "l_")
        PW = P + W
        z = sb("z", [P, NT, P])
        xt = sb("xt", [P, S])
        qp = sb("qp", [P, 2, H, S])
        kt = sb("kt", [P, 2, HP, S])
        vv = sb("vv", [P, 2, NT, 2, HP, DH])
        vs = sb("vs", [P, 2, NT, HP, DH])
        mx = sb("mx", [P, HU])
        nb = sb("nb", [P, 2, HU])
        sums = sb("sums", [P, 2, HU])
        rs = sb("rs", [P, 2, HU])
        p = sb("p", [P, 2, HU, PW])
        pn = sb("pn", [P, 2, HU * PW])
        pt = sb("pt", [P, 2, HU * PW])
        ot = sb("ot", [P, 2, HP, P])
        ones = sb("ones", [1, W])
        none = sb("none", [1, 2 * W])
        sm = ps("sm", [P, 2, 2, BANK])
        tp = ps("tp", [P, 2 * BANK])
        xb = ps("xb", [P, BANK])
        pj = ps("pj", [P, BANK])
        XO = HU // 2 * P
        SCALE = float(DH) ** -0.5

        s_i = sem("i")
        s_z = sem("z")
        s_pp = sem("pp")
        s_pe = sem("pe")
        s_vs = sem("vs")
        s_sm = sem("sm")
        s_mx = sem("mx")
        s_nb = sem("nb")
        s_ex = sem("ex")
        s_rs = sem("rs")
        s_nm = sem("nm")
        s_t = sem("t")
        s_pt = sem("pt")
        s_pv = sem("pv")
        s_oe = sem("oe")
        s_w = sem("w")
        s_la = sem("la")
        s_sc = sem("sc")
        s_sk = sem("sk")
        s_sl = sem("sl")
        USES = 1 + 2 * HP + NT
        RSTEPS = (1, 3, 5)
        work = ctx.enter_context(ExitStack())
        block = work.enter_context(nc.Block())

        def near(b, par, u, k):
            v = u + k
            if v < 0:
                return b - 1, 1 - par, v + UNITS
            if v >= UNITS:
                return b + 1, 1 - par, v - UNITS
            return b, par, v

        def exists(b, u, k):
            return not (isinstance(b, int) and (b * UNITS + u + k < 0 or b * UNITS + u + k >= B * UNITS))

        def bank(b, k):
            return (pj[:], tp[:, 0:BANK], tp[:, BANK:], xb[:])[k % 4 if isinstance(b, int) and b == 0 else 0]

        @block.sync
        def _(sp):
            def batch(b, par):
                sp.wait_ge(s_pe, USES * (b + 1))
                apart(sp)
                wait(sp, s_pv, UNITS * (b - 1))
                apart(sp)
                sp.dma_start(vs[0:64, par], vv[64:P, par, :, 0]).then_inc(s_vs, 16)
                sp.dma_start(vs[64:P, par], vv[0:64, par, :, 1]).then_inc(s_vs, 16)
                sp.wait_ge(s_vs, 32 * (b + 1))
                apart(sp)

            in_pairs(sp, lambda i: [batch(2 * i + e, e) for e in range(2)])

        @block.tensor
        def _(pe):
            def use(b, par, k):
                first = isinstance(b, int) and b == 0
                at = bank(b, k)
                wait(pe, s_pe, max(k - 3, min(k, 1)) if first else USES * b + k)
                if k == 0:
                    pe.wait_ge(s_z, b + 1)
                    for j in range(NT):
                        mm = nc.tensor.transpose(at[:, j * P:(j + 1) * P], z[:, j, :], K["ident"][:])
                elif k <= 2 * HP:
                    mm = nc.tensor.matmul(at, K["wqkv"][:, (k - 1) * P:k * P], xt[:], start=True, stop=True)
                else:
                    j = k - 1 - 2 * HP
                    mm = nc.tensor.matmul(at, xt[:, j * P:(j + 1) * P], K["wqkv"][:, 2 * H * DH:3 * H * DH],
                                          start=True, stop=True)
                mm.then_inc(s_pp, 1)

            def scores(b, par, u):
                n = UNITS * b + u
                i, g = u // 2, u % 2
                if u == 0:
                    pe.wait_ge(s_pe, USES * b + 1 + 2 * HP)
                wait(pe, s_ex, n - 1)
                for half, there in ((0, i > 0), (1, i < NT - 1)):
                    if not there:
                        for c in range(HU // 2):
                            nc.tensor.matmul(sm[64 * half:64 * half + 64, u % 2, c, 0:2 * PW]
                                             .rearrange("p (h k) -> p h k", h=2)[:, :, P:],
                                             ones[:], none[:].rearrange("p (h k) -> p h k", h=2),
                                             start=True, stop=True)
                for k in range(HU):
                    h = HU * g + k
                    out = sm[:, u % 2, k // 2, k % 2 * PW:(k % 2 + 1) * PW]
                    keys = kt[:, par, h // 2, :]
                    if i > 0:
                        nc.tensor.matmul(out[0:64, P:], qp[:, par, h, i * P:i * P + W], keys[:, i * P - W:i * P],
                                         start=True, stop=True)
                    if i < NT - 1:
                        nc.tensor.matmul(out[64:P, P:], qp[:, par, h, i * P + W:(i + 1) * P],
                                         keys[:, (i + 1) * P:(i + 1) * P + W], start=True, stop=True)
                    mm = nc.tensor.matmul(out[:, 0:P], qp[:, par, h, i * P:(i + 1) * P], keys[:, i * P:(i + 1) * P],
                                          start=True, stop=True)
                mm.then_inc(s_sm, 1)

            def turn(b, par, u):
                n = UNITS * b + u
                pe.wait_ge(s_nm, n + 1)
                wait(pe, s_pt, n)
                for k in range(HU + HU // 2):
                    at = slice(k * P, (k + 1) * P)
                    mm = nc.tensor.transpose(tp[:, at], pn[:, u % 2, at], K["ident"][:])
                mm.then_inc(s_t, 1)

            def values(b, par, u):
                n = UNITS * b + u
                i, g = u // 2, u % 2
                if u == 0:
                    pe.wait_ge(s_vs, 32 * (b + 1))
                if u % 2 == 0:
                    wait(pe, s_la, NT * b + i)
                wait(pe, s_oe, n)
                pe.wait_ge(s_pt, n + 1)
                for cc in range(HU // 2):
                    c = HU // 2 * g + cc
                    for e in range(2):
                        k = 2 * cc + e
                        nc.tensor.matmul(xb[64 * e:64 * e + 64, cc * P:(cc + 1) * P], vv[:, par, i, e, c, :],
                                         pt[:, u % 2, k * P:(k + 1) * P], start=True, stop=False,
                                         skip_group_check=True)
                    for half, j in ((0, i - 1), (1, i + 1)):
                        for e in range(2):
                            if 0 <= j < NT:
                                rows = slice(64 * e, 64 * e + 64)
                                v = vs[rows, par, j, c, :] if e == half else vv[rows, par, j, e, c, :]
                                at = cc * P + half * W
                                mm = nc.tensor.matmul(xb[rows, at:at + W], v,
                                                      pt[rows, u % 2, HU * P + at:HU * P + at + W],
                                                      start=False, stop=True, skip_group_check=True)
                mm.then_inc(s_pv, 1)

            def output(t, tpar):
                pe.wait_ge(s_oe, 2 * t + 2)
                for c in range(HP):
                    mm = nc.tensor.matmul(xb[:, XO:XO + P], ot[:, tpar, c, :], K["wout_l"][:, c * P:(c + 1) * P],
                                          start=(c == 0), stop=(c == HP - 1))
                mm.then_inc(s_w, 1)

            for k in range(USES):
                use(0, 0, k)
            pe.wait_ge(s_i, 2)
            scores(0, 0, 0)

            def slot(b, par, u):
                last = isinstance(b, int) and b == B - 1
                if exists(b, u, 1):
                    scores(*near(b, par, u, 1))
                if u % 2 == 0 and exists(b, u, -2):
                    output(NT * b + u // 2 - 1, (u // 2 - 1) % 2)
                if 2 * u < USES and not last:
                    use(b + 1, 1 - par, 2 * u)
                turn(b, par, u)
                if 2 * u + 1 < USES and not last:
                    use(b + 1, 1 - par, 2 * u + 1)
                values(b, par, u)

            in_pairs(pe, lambda i: [slot(2 * i + e, e, u) for e in range(2) for u in range(UNITS)])
            output(T - 1, 1)

        @block.scalar
        def _(act):
            def leave(b, par, k):
                act.wait_ge(s_pp, USES * b + k + 1)
                at = bank(b, k)
                if k == 0:
                    ins = nc.scalar.activation(xt[:], at, ACT.Identity, scale=K["ln_w"][:, 0:1],
                                               bias=K["ln_b"][:, 0:1])
                elif k <= HP:
                    c = k - 1
                    nc.scalar.activation(qp[0:64, par, 2 * c, :], at[0:64, :], ACT.Copy)
                    ins = nc.scalar.activation(qp[64:P, par, 2 * c + 1, :], at[64:P, :], ACT.Copy)
                elif k <= 2 * HP:
                    ins = nc.scalar.activation(kt[:, par, k - 1 - HP, :], at, ACT.Copy)
                else:
                    ins = nc.scalar.activation(vv[:, par, k - 1 - 2 * HP],
                                               at.rearrange("p (c e d) -> p e c d", c=HP, e=2), ACT.Copy)
                ins.then_inc(s_pe, 1)

            def exps(b, par, u):
                n = UNITS * b + u
                act.wait_ge(s_nb, n + 1)
                wait(act, s_nm, n - 1)
                for k in range(HU):
                    ins = nc.scalar.activation(p[:, u % 2, k, :], sm[:, u % 2, k // 2, k % 2 * PW:(k % 2 + 1) * PW],
                                               ACT.Exp, bias=nb[:, u % 2, k:k + 1], scale=SCALE,
                                               accum_out=sums[:, u % 2, k:k + 1])
                ins.then_inc(s_ex, 1)

            def leave_values(b, par, u):
                n = UNITS * b + u
                act.wait_ge(s_pv, n + 1)
                if u % 2 == 0:
                    wait(act, s_w, NT * b + u // 2 - 1)
                g = u % 2
                nc.scalar.activation(ot[:, u // 2 % 2, g * HU // 2:(g + 1) * HU // 2, :],
                                     xb[:, 0:XO].rearrange("p (c q) -> p c q", q=P), ACT.Copy).then_inc(s_oe, 1)

            def route(k):
                act.wait_ge(s_sk, k + 1)
                nc.scalar.activation(K["shift"][:], K["shift"][:], ACT.Exp, accum_out=K["sum"][:]).then_inc(s_sl, 1)
                act.wait_ge(s_sl, 2 * k + 1)
                nc.scalar.activation(K["lns"][:], K["sum"][:], ACT.Ln).then_inc(s_sl, 1)

            nc.scalar.preload_act_table_set("natural_log_exp_and_others")
            for k in range(USES):
                if k == 1:
                    act.wait_ge(s_i, 1)
                leave(0, 0, k)
            act.wait_ge(s_i, 2)
            exps(0, 0, 0)

            def slot(b, par, u):
                last = isinstance(b, int) and b == B - 1
                if exists(b, u, -1):
                    leave_values(*near(b, par, u, -1))
                if 2 * u < USES and not last:
                    leave(b + 1, 1 - par, 2 * u)
                if exists(b, u, 1):
                    exps(*near(b, par, u, 1))
                if 2 * u + 1 < USES and not last:
                    leave(b + 1, 1 - par, 2 * u + 1)
                if u in RSTEPS:
                    route(len(RSTEPS) * b + RSTEPS.index(u))

            in_pairs(act, lambda i: [slot(2 * i + e, e, u) for e in range(2) for u in range(UNITS)])
            leave_values(B - 1, 1, UNITS - 1)

        @block.vector
        def _(dve):
            def maxima(b, par, u):
                n = UNITS * b + u
                dve.wait_ge(s_sm, n + 1)
                nc.vector.tensor_reduce(mx[:], sm[:, u % 2, :, 0:2 * PW].rearrange("p a (k c) -> p a k c", k=2), AX,
                                        ALU.max).then_inc(s_mx, 1)
                dve.wait_ge(s_mx, n + 1)
                nc.vector.tensor_scalar(nb[:, u % 2, :], mx[:], -SCALE, None, ALU.mult).then_inc(s_nb, 1)

            def reciprocals(b, par, u):
                n = UNITS * b + u
                dve.wait_ge(s_ex, n + 1)
                wait(dve, s_nm, n - 1)
                nc.vector.reciprocal(rs[:, u % 2, :], sums[:, u % 2, :]).then_inc(s_rs, 1)

            def leave_turned(b, par, u):
                n = UNITS * b + u
                dve.wait_ge(s_t, n + 1)
                wait(dve, s_pv, n - 1)
                nc.vector.tensor_copy(pt[:, u % 2, :], tp[:, 0:HU * PW]).then_inc(s_pt, 1)

            def residual(t):
                dve.wait_ge(s_w, t + 1)
                nc.vector.tensor_tensor(K["x"][:, t, :], K["x"][:, t, :], xb[:, XO:XO + P], ALU.add).then_inc(s_la, 1)

            def route_shift(k):
                wait(dve, s_sc, 2 * k)
                nc.vector.tensor_tensor(K["m"][:], K["smax"][:], K["na"][:], ALU.min).then_inc(s_sc, 1)
                dve.wait_ge(s_sc, 2 * k + 1)
                nc.vector.tensor_scalar(K["shift"][:], K["srow"][:], K["na"][:, 0:1], K["m"][:, 0:1],
                                        ALU.min, ALU.subtract).then_inc(s_sk, 1)

            def route_step(k):
                dve.wait_ge(s_sl, 2 * k + 2)
                nc.vector.scalar_tensor_tensor(K["na"][:], K["lns"][:], K["m"][:, 0:1],
                                               K["router_rows"][0:2 * B, 0:1], ALU.add, ALU.add).then_inc(s_sc, 1)

            maxima(0, 0, 0)
            reciprocals(0, 0, 0)

            def slot(b, par, u):
                if exists(b, u, 1):
                    maxima(*near(b, par, u, 1))
                if u % 2 == 0 and exists(b, u, -2):
                    residual(NT * b + u // 2 - 1)
                leave_turned(b, par, u)
                if u - 1 in RSTEPS:
                    route_step(len(RSTEPS) * b + RSTEPS.index(u - 1))
                if exists(b, u, 1):
                    reciprocals(*near(b, par, u, 1))
                if u in RSTEPS:
                    route_shift(len(RSTEPS) * b + RSTEPS.index(u))

            in_pairs(dve, lambda i: [slot(2 * i + e, e, u) for e in range(2) for u in range(UNITS)])
            residual(T - 1)

        @block.gpsimd
        def _(pool):
            def scaled(b):
                wait(pool, s_pp, USES * (b - 1) + 1)
                t = bass.ds(b * NT, NT)
                nc.gpsimd.tensor_tensor(z[:], K["y"][:, t, :],
                                        K["r2"][:, t].unsqueeze(2).broadcast_to([P, NT, P]), ALU.mult).then_inc(s_z, 1)

            def normalise(b, par, u):
                n = UNITS * b + u
                pool.wait_ge(s_rs, n + 1)
                wait(pool, s_t, n - 1)
                r = rs[:, u % 2, :].unsqueeze(2)
                for cols, at in ((slice(0, P), 0), (slice(P, PW), HU * P)):
                    w = cols.stop - cols.start
                    ins = nc.gpsimd.tensor_tensor(pn[:, u % 2, at:at + HU * w].rearrange("p (k c) -> p k c", k=HU),
                                                  p[:, u % 2, :, cols], r.broadcast_to([P, HU, w]), ALU.mult)
                ins.then_inc(s_nm, 1)

            scaled(0)
            nc.gpsimd.memset(ones[:], 1.0)
            nc.gpsimd.memset(none[:], -1e9 / SCALE)
            nc.gpsimd.memset(qp[:, 0], 0.0).then_inc(s_i, 1)
            nc.gpsimd.memset(qp[:, 1], 0.0).then_inc(s_i, 1)
            scaled(1)
            normalise(0, 0, 0)

            def slot(b, par, u):
                if exists(b, u, 1):
                    normalise(*near(b, par, u, 1))
                if u == 5 and not (isinstance(b, int) and b >= B - 2):
                    scaled(b + 2)

            in_pairs(pool, lambda i: [slot(2 * i + e, e, u) for e in range(2) for u in range(UNITS)])

        work.close()
        sem.end()


def stage_topk(nc, K, tag):
    with ExitStack() as ctx:
        sb = lambda n, s, d=F32: ctx.enter_context(nc.sbuf_tensor(tag + "k_" + n, s, d))
        sem = Semaphores(nc, ctx, tag + "k_")
        R2 = 2 * B
        w = sb("w", [R2, S])
        m8 = sb("m8", [R2, S])
        one = sb("one", [R2, S])
        top = sb("top", [R2, 8])
        pp = ctx.enter_context(nc.psum_tensor(tag + "k_pp", [P, BANK], F32))
        s_d, s_a, s_p, s_pl = sem("d"), sem("a"), sem("p"), sem("pl")
        work = ctx.enter_context(ExitStack())
        block = work.enter_context(nc.Block())
        R = K["router_rows"]

        @block.vector
        def _(dve):
            link = Chain(dve, s_d)
            link(nc.vector.tensor_scalar(w[:], K["srow"][:], K["na"][:, 0:1], 0.0, ALU.subtract, ALU.min))
            dve.wait_ge(s_a, 1)
            for r in range(NKV // 8):
                link(nc.vector.max(top[:], w[:]))
                link(nc.vector.match_replace(w[:], top[:], w[:], -1.0))
                if r == NQ // 8 - 1:
                    link(nc.vector.tensor_scalar(m8[:], w[:], 0.0, None, ALU.is_lt))
            link(nc.vector.tensor_scalar(w[:], w[:], 0.0, None, ALU.is_lt))
            link(nc.vector.scalar_tensor_tensor(w[:], m8[:], R[0:R2, 3:4], w[:], ALU.max, ALU.min))
            dve.wait_ge(s_pl, 1)
            link(nc.vector.tensor_tensor_scan(m8[:], one[:], w[:], 0.0, ALU.mult, ALU.add))
            link(nc.vector.scalar_tensor_tensor(m8[:], m8[:], R[0:R2, 2:3], w[:], ALU.subtract, ALU.mult))
            link(nc.vector.tensor_scalar(m8[:], m8[:], R[0:R2, 1:2], None, ALU.add))
            dve.wait_ge(s_p, 1)
            nc.vector.tensor_copy(K["place"][:], pp[:, 0:NT * R2].rearrange("p (j r) -> p j r", j=NT))

        @block.scalar
        def _(act):
            act.wait_ge(s_d, 1)
            nc.scalar.activation(w[:], w[:], ACT.Exp).then_inc(s_a, 1)

        @block.gpsimd
        def _(pool):
            nc.gpsimd.memset(one[:], 1.0).then_inc(s_pl, 1)

        @block.tensor
        def _(pe):
            pe.wait_ge(s_d, 1 + 2 * (NKV // 8) + 1 + 5)
            for j in range(NT):
                mm = nc.tensor.transpose(pp[:, j * R2:(j + 1) * R2], m8[:, j * P:(j + 1) * P], K["ident"][0:R2, 0:R2])
            mm.then_inc(s_p, 1)

        work.close()
        sem.end()


def stage_heavy(nc, K, tag, stats):
    with ExitStack() as ctx:
        sb = lambda n, s, d=F32: ctx.enter_context(nc.sbuf_tensor(tag + "h_" + n, s, d))
        sem = Semaphores(nc, ctx, tag + "h_")
        GC = NQ + 1 + NKV
        yb = sb("yb", [P, 2, NT, P])
        g = sb("g", [P, 2, NT, GC])
        gx = sb("gx", [P, 2, GC])
        gt = sb("gt", [NQ + 1, 2, 2, S])
        K1 = NKV + 1
        qp = sb("qp", [P, 2, H, NQ])
        kt = sb("kt", [P, 2, HP, K1])
        vv = sb("vv", [P, 2, H, DH])
        mx = sb("mx", [P, 2, HP])
        nb = sb("nb", [P, 2, HP])
        sums = sb("sums", [P, 2, HP])
        rs = sb("rs", [P, 2, HP])
        pr = sb("pr", [P, 2, HP, K1])
        pt = sb("pt", [P, 2, HP, 2, NQ])
        pz = sb("pz", [HP, 2, 2, NQ])
        ot = sb("ot", [P, 2, HP, NQ])
        hv = sb("hv", [NQ + 1, 2, E])
        st6 = sb("st6", [P, 2, NT, 6])
        mv4 = sb("mv4", [P, 2, NT, 2])
        W_ = ctx.enter_context(nc.psum_tensor(tag + "h_ps", [P, 2, 4, BANK], F32))

        s_i = sem("i")
        s_iv = sem("iv")
        s_y = sem("y")
        s_g = sem("g")
        p_g = sem("pg")
        p_t = sem("pt")
        a_x = sem("ax")
        v_t = sem("vt")
        p_q = sem("pq")
        p_k = sem("pk")
        p_v = sem("pv")
        a_q = sem("aq")
        a_k = sem("ak")
        v_v = sem("vv")
        p_r = sem("pr")
        v_m = sem("vm")
        a_e = sem("ae")
        v_r = sem("vr")
        p_n = sem("pn")
        v_p = sem("vp")
        p_o = sem("po")
        a_ot = sem("aot")
        p_h = sem("ph")
        v_h = sem("vh")
        p_x = sem("px")
        v_x = sem("vx")
        v_s = sem("vs")
        SCALE = float(DH) ** -0.5
        work = ctx.enter_context(ExitStack())
        block = work.enter_context(nc.Block())

        def both(step):
            return lambda i: [step(2 * i + e, e) for e in range(2)]

        def begun(i):
            return not (isinstance(i, int) and i == 0)

        @block.tensor
        def _(pe):
            def gather(b, e):
                pe.wait_ge(s_y, b + 1)
                pe.wait_ge(s_g, b + 1)
                wait(pe, a_ot, b - 1)
                for j in range(NT):
                    mm = nc.tensor.matmul(W_[:, e, 0, 0:GC], yb[:, e, j, :], g[:, e, j, :],
                                          start=(j == 0), stop=(j == NT - 1))
                mm.then_inc(p_g, 1)
                for j in range(NT):
                    mm = nc.tensor.transpose(W_[0:NQ + 1, e, 1, j * P:(j + 1) * P], g[:, e, j, 0:NQ + 1],
                                             K["ident"][:])
                mm.then_inc(p_t, 1)

            def project(b, e):
                pe.wait_ge(a_x, b + 1)
                for c in range(HP):
                    mm = nc.tensor.matmul(W_[:, e, 2, c * NQ:(c + 1) * NQ], K["wq_h"][:, c * P:(c + 1) * P],
                                          gx[:, e, 0:NQ], start=True, stop=True)
                mm.then_inc(p_q, 1)
                for c in range(HP):
                    mm = nc.tensor.matmul(W_[:, e, 0, c * P:(c + 1) * P], K["wk_h"][:, c * P:(c + 1) * P],
                                          gx[:, e, NQ + 1:], start=True, stop=True)
                mm.then_inc(p_k, 1)
                nc.tensor.matmul(W_[:, e, 3, :], gx[:, e, NQ + 1:], K["wv_h"][:], start=True, stop=True).then_inc(p_v, 1)

            def scores(b, e):
                pe.wait_ge(a_q, b + 1)
                pe.wait_ge(a_k, b + 1)
                pe.wait_ge(v_t, b + 1)
                for c in range(HP):
                    mm = nc.tensor.matmul(W_[:, e, c // 2, c % 2 * K1:(c % 2 + 1) * K1],
                                          qp[:, e, 2 * c:2 * c + 2, :].rearrange("p h q -> p (h q)"), kt[:, e, c, :],
                                          start=True, stop=True)
                mm.then_inc(p_r, 1)

            def turn(b, e):
                pe.wait_ge(v_r, 2 * b + 2)
                pe.wait_ge(v_v, b + 1)
                wait(pe, v_x, b - 1)
                for c in range(HP):
                    nc.tensor.transpose(W_[:, e, 2, c * P:(c + 1) * P], pr[:, e, c, 0:NKV], K["ident"][:])
                nc.tensor.transpose(W_[0:HP, e, 3, 0:P], pr[:, e, :, NKV], K["ident"][:]).then_inc(p_n, 1)

            def values(b, e):
                pe.wait_ge(v_p, b + 1)
                for c in range(HP):
                    for o in range(2):
                        out = W_[64 * o:64 * o + 64, e, 0, c * NQ:(c + 1) * NQ]
                        nc.tensor.matmul(out, vv[:, e, 2 * c + o, :], pt[:, e, c, o, :], start=True, stop=False,
                                         skip_group_check=True)
                        mm = nc.tensor.matmul(out, K["null_v"][0:HP, (2 * c + o) * DH:(2 * c + o + 1) * DH],
                                              pz[:, e, o, :], start=False, stop=True, skip_group_check=True)
                mm.then_inc(p_o, 1)

            def output(b, e, more=True):
                pe.wait_ge(a_ot, b + 1)
                pe.wait_ge(v_v, b + 3 if more else b + 1)
                for c in range(HP):
                    mm = nc.tensor.matmul(W_[0:NQ, e, 3, 0:E], ot[:, e, c, :], K["wout_h"][:, c * E:(c + 1) * E],
                                          start=(c == 0), stop=(c == HP - 1))
                mm.then_inc(p_h, 1)

            def scatter(b, e, par):
                pe.wait_ge(v_h, b + 1)
                for j in range(NT):
                    mm = nc.tensor.matmul(W_[:, e, 2, j * P:(j + 1) * P], gt[:, par, e, j * P:(j + 1) * P], hv[:, e, :],
                                          start=True, stop=True)
                mm.then_inc(p_x, 1)

            pe.wait_ge(s_i, 2)
            pe.wait_ge(s_iv, 1)
            def pair(i, par):
                for s in (gather, project, scores):
                    both(s)(i)
                if begun(i):
                    both(output)(i - 1)
                    both(lambda b, e: scatter(b, e, 1 - par))(i - 1)
                for s in (turn, values):
                    both(s)(i)

            in_fours(pe, pair)
            both(lambda b, e: output(b, e, False))(B // 2 - 1)
            both(lambda b, e: scatter(b, e, 1))(B // 2 - 1)

        @block.scalar
        def _(act):
            def tokens(b, e):
                act.wait_ge(p_g, b + 1)
                wait(act, p_v, b - 1)
                nc.scalar.activation(gx[:, e, :], W_[:, e, 0, 0:GC], ACT.Copy,
                                     scale=K["gam_h"][:, 0:1]).then_inc(a_x, 1)

            def queries(b, e):
                act.wait_ge(p_q, b + 1)
                v = W_[:, e, 2, 0:HP * NQ].rearrange("p (c q) -> p c q", c=HP)
                q = qp[:, e].rearrange("p (c o) q -> p c o q", o=2)
                nc.scalar.activation(q[0:64, :, 0, :], v[0:64], ACT.Copy)
                nc.scalar.activation(q[64:P, :, 1, :], v[64:P], ACT.Copy).then_inc(a_q, 1)

            def keys(b, e):
                act.wait_ge(p_k, b + 1)
                nc.scalar.activation(kt[:, e, :, 0:NKV], W_[:, e, 0, :].rearrange("p (c k) -> p c k", c=HP),
                                     ACT.Copy).then_inc(a_k, 1)

            def exps(b, e):
                act.wait_ge(v_m, 2 * b + 2)
                for c in range(HP):
                    ins = nc.scalar.activation(pr[:, e, c, :], W_[:, e, c // 2, c % 2 * K1:(c % 2 + 1) * K1], ACT.Exp,
                                               bias=nb[:, e, c:c + 1], scale=SCALE, accum_out=sums[:, e, c:c + 1])
                ins.then_inc(a_e, 1)

            def values(b, e):
                act.wait_ge(p_o, b + 1)
                nc.scalar.activation(ot[:, e], W_[:, e, 0, 0:HP * NQ].rearrange("p (c q) -> p c q", c=HP),
                                     ACT.Copy).then_inc(a_ot, 1)

            act.wait_ge(s_i, 2)
            act.wait_ge(s_iv, 1)
            in_pairs(act, lambda i: [both(s)(i) for s in (tokens, queries, keys, exps, values)])

        @block.gpsimd
        def _(pool):
            nc.gpsimd.memset(qp[:, 0], 0.0).then_inc(s_i, 1)
            nc.gpsimd.memset(qp[:, 1], 0.0).then_inc(s_i, 1)

            def scaled(b, e):
                wait(pool, p_g, b - 1)
                t = bass.ds(b * NT, NT)
                nc.gpsimd.tensor_tensor(yb[:, e], K["y"][:, t, :], K["rc"][:, t].unsqueeze(2).broadcast_to([P, NT, P]),
                                        ALU.mult).then_inc(s_y, 1)

            in_pairs(pool, both(scaled))

        @block.vector
        def _(dve):
            for e in range(2):
                nc.vector.tensor_copy(kt[:, e, :, NKV:], K["null_k"][:].unsqueeze(2))
                ins = nc.vector.tensor_copy(hv[NQ:NQ + 1, e, :], K["null_q"][:])
            ins.then_inc(s_iv, 1)

            def onehots(b, e):
                wait(dve, p_t, b - 1)
                place = lambda r: K["place"][:, :, bass.ds(r, 1)]
                nc.vector.tensor_tensor(g[:, e, :, 0:NQ + 1],
                                        K["iota"][:, 0:NQ + 1].unsqueeze(1).broadcast_to([P, NT, NQ + 1]),
                                        place(b).broadcast_to([P, NT, NQ + 1]), ALU.is_equal)
                nc.vector.tensor_tensor(g[:, e, :, NQ + 1:],
                                        K["iota"][:, NQ + 1:].unsqueeze(1).broadcast_to([P, NT, NKV]),
                                        place(b + B).broadcast_to([P, NT, NKV]), ALU.is_equal).then_inc(s_g, 1)

            def turned(b, e, par):
                dve.wait_ge(p_t, b + 1)
                wait(dve, p_x, b - 3)
                nc.vector.tensor_copy(gt[:, par, e, :], W_[0:NQ + 1, e, 1, :]).then_inc(v_t, 1)

            def values(b, e):
                dve.wait_ge(p_v, b + 1)
                nc.vector.tensor_copy(vv[:, e], W_[:, e, 3, :].rearrange("p (h d) -> p h d", h=H)).then_inc(v_v, 1)

            def maxima(b, e):
                dve.wait_ge(p_r, b + 1)
                nc.vector.tensor_reduce(mx[:, e].rearrange("p (a k) -> p a k", a=2),
                                        W_[:, e, 0:2, 0:2 * K1].rearrange("p a (k c) -> p a k c", k=2),
                                        AX, ALU.max).then_inc(v_m, 1)
                dve.wait_ge(v_m, 2 * b + 1)
                nc.vector.tensor_scalar(nb[:, e], mx[:, e], -SCALE, None, ALU.mult).then_inc(v_m, 1)

            def normalise(b, e):
                dve.wait_ge(a_e, b + 1)
                nc.vector.reciprocal(rs[:, e], sums[:, e]).then_inc(v_r, 1)
                dve.wait_ge(v_r, 2 * b + 1)
                nc.vector.tensor_tensor(pr[:, e], pr[:, e], rs[:, e].unsqueeze(2).broadcast_to([P, HP, K1]),
                                        ALU.mult).then_inc(v_r, 1)

            def turned_probabilities(b, e):
                dve.wait_ge(p_n, b + 1)
                nc.vector.tensor_copy(pt[:, e].rearrange("p c o q -> p (c o q)"), W_[:, e, 2, :])
                nc.vector.tensor_copy(pz[:, e].rearrange("p o q -> p (o q)"), W_[0:HP, e, 3, 0:P]).then_inc(v_p, 1)

            def heavy(b, e):
                dve.wait_ge(p_h, b + 1)
                nc.vector.tensor_copy(hv[0:NQ, e, :], W_[0:NQ, e, 3, 0:E]).then_inc(v_h, 1)

            def residual(b, e):
                dve.wait_ge(p_x, b + 1)
                xb = K["x"][:, bass.ds(b * NT, NT), :]
                nc.vector.tensor_tensor(xb, xb, W_[:, e, 2, :].rearrange("p (j d) -> p j d", j=NT), ALU.add).then_inc(v_x, 1)

            def statistics(b, e):
                dve.wait_ge(v_x, b + 1)
                apart(dve)
                for j in range(NT):
                    ins = nc.vector.bn_stats(st6[:, e, j, :], K["x"][:, b * NT + j, :])
                ins.then_inc(v_s, 1)
                dve.wait_ge(v_s, 3 * b + 1)
                apart(dve)
                for j in range(NT):
                    ins = nc.vector.bn_aggr(mv4[:, e, j, :], st6[:, e, j, :])
                ins.then_inc(v_s, 1)
                dve.wait_ge(v_s, 3 * b + 2)
                nc.vector.tensor_copy(K["mv"][:, bass.ds(b * NT, NT), :], mv4[:, e]).then_inc(v_s, 1)

            onehots(0, 0)
            onehots(1, 1)

            def pair(i, par):
                both(lambda b, e: turned(b, e, par))(i)
                both(values)(i)
                both(maxima)(i)
                if begun(i):
                    both(heavy)(i - 1)
                    both(residual)(i - 1)
                both(normalise)(i)
                both(turned_probabilities)(i)
                if not (isinstance(i, int) and i == B // 2 - 1):
                    both(onehots)(i + 1)
                if begun(i) and stats:
                    both(statistics)(i - 1)

            in_fours(dve, pair)
            both(heavy)(B // 2 - 1)
            both(residual)(B // 2 - 1)
            if stats:
                both(statistics)(B // 2 - 1)

        work.close()
        sem.end()


def stage_ssm(nc, K):
    with ExitStack() as ctx:
        sb = lambda n, s, d=F32: ctx.enter_context(nc.sbuf_tensor("s_" + n, s, d))
        ps = lambda n, s, d=F32: ctx.enter_context(nc.psum_tensor("s_" + n, s, d))
        sem = Semaphores(nc, ctx, "s_")
        c = {n: sb("c_" + n, [P, 1]) for n in ("dt", "mag", "th", "n", "sin", "cos", "t", "lr", "li", "den",
                                               "fr", "fi", "ck", "sk", "ck2", "sk2")}
        bb = sb("bb", [P, P])
        bbt = sb("bbt", [P, P])
        cc = sb("cc", [P, S])
        ss = sb("ss", [P, S])
        tmp = sb("tmp", [P, S])
        dec = sb("dec", [P, S])
        g1 = sb("g1", [P, 2, P])
        g2 = sb("g2", [P, 2, P])
        dd = sb("dd", [P, P])
        vy = sb("vy", [P, T])
        r3 = sb("r3", [P, T])
        xn = sb("xn", [P, 2, 2, NT, P])
        un = sb("un", [P, 2, 2, NT, P])
        ut = sb("ut", [P, 2, 2, S])
        t1 = sb("t1", [P, S])
        t2 = sb("t2", [P, S])
        wi = sb("wi", [P, S])
        wo = sb("wo", [P, S])
        v1 = sb("v1", [P, S])
        v2 = sb("v2", [P, S])
        st6 = sb("st6", [P, 2 * NT, 6])
        mv8 = sb("mv8", [P, 2 * NT, 2])
        tp = ps("tp", [P, 2, BANK])
        xx = ps("xx", [P, 2, BANK])
        yy = ps("yy", [P, 2, BANK])

        s_d = sem("d")
        s_a = sem("a")
        s_b = sem("b")
        s_xn = sem("xn")
        s_un = sem("un")
        s_xx = sem("xxn")
        s_t = sem("t")
        s_te = sem("te")
        s_x = sem("x")
        s_r = sem("r")
        s_w = sem("w")
        s_s = sem("s")
        s_y = sem("y")
        s_o = sem("o")
        s_st = sem("st")
        work = ctx.enter_context(ExitStack())
        block = work.enter_context(nc.Block())
        HALF_PI = float(np.float32(np.pi / 2))
        TURN = 2 * np.pi
        T1 = 6.28125
        T2 = float(np.float32(int((TURN - T1) * 2 ** 21) / 2 ** 21))
        T3 = float(np.float32(TURN - T1 - T2))
        ROUND = float(1.5 * 2 ** 23)
        sign = K["ssm_sign"]

        @block.vector
        def _(dve):
            v = nc.vector
            link = Chain(dve, s_d)
            link(v.tensor_scalar(K["rstd"][:], K["mv"][:, :, 1], 1e-5, None, ALU.add))
            dve.wait_ge(s_a, 1)
            link(v.reciprocal(K["rstd"][:], K["rstd"][:]))
            link(v.tensor_tensor(vy[:], K["mv"][:, :, 1], K["rstd"][:], ALU.mult))
            link(v.tensor_tensor(vy[:], vy[:], K["rstd"][:], ALU.mult))
            link(v.tensor_scalar(r3[:], vy[:], 1e-6, None, ALU.add))
            dve.wait_ge(s_a, 2)
            link(v.reciprocal(r3[:], r3[:]))

            def norm(p, par):
                wait(dve, s_un, p - 1)
                wait(dve, s_xx, p - 1)
                for e in range(2):
                    for j in range(NT):
                        t = (2 * p + e) * NT + j
                        ins = v.tensor_scalar(xn[:, par, e, j, :], K["x"][:, t, :], K["mv"][:, t, 0:1],
                                              K["rstd"][:, bass.ds(t, 1)], ALU.subtract, ALU.mult)
                ins.then_inc(s_xn, 1)

            norm(0, 0)
            dve.wait_ge(s_a, 3)
            link(v.tensor_tensor(c["t"][:], K["lam_re"][:], c["dt"][:], ALU.mult))
            link(v.tensor_tensor(c["th"][:], K["lam_im"][:], c["dt"][:], ALU.mult))
            link(v.tensor_scalar(c["n"][:], c["th"][:], float(1 / TURN), ROUND, ALU.mult, ALU.add))
            link(v.tensor_scalar(c["n"][:], c["n"][:], ROUND, None, ALU.subtract))
            for part in (T1, T2, T3):
                link(v.scalar_tensor_tensor(c["th"][:], c["n"][:], -part, c["th"][:], ALU.mult, ALU.add))
            link(v.tensor_scalar(c["n"][:], c["th"][:], HALF_PI, -TURN, ALU.is_gt, ALU.mult))
            link(v.scalar_tensor_tensor(c["n"][:], c["th"][:], HALF_PI, c["n"][:], ALU.add, ALU.add))
            link(v.tensor_scalar(c["th"][:], c["th"][:], 3.1415925, -3.1415925, ALU.min, ALU.max))
            link(v.tensor_scalar(c["n"][:], c["n"][:], 3.1415925, -3.1415925, ALU.min, ALU.max))
            dve.wait_ge(s_a, 6)
            link(v.tensor_scalar(c["lr"][:], c["cos"][:], c["mag"][:, 0:1], -1.0, ALU.mult, ALU.add))
            link(v.tensor_tensor(c["li"][:], c["sin"][:], c["mag"][:], ALU.mult))
            link(v.tensor_tensor(c["den"][:], K["lam_re"][:], K["lam_re"][:], ALU.mult))
            link(v.scalar_tensor_tensor(c["den"][:], K["lam_im"][:], K["lam_im"][:, 0:1], c["den"][:], ALU.mult, ALU.add))
            link(v.reciprocal(c["den"][:], c["den"][:]))
            link(v.tensor_tensor(c["t"][:], c["li"][:], K["lam_im"][:], ALU.mult))
            link(v.scalar_tensor_tensor(c["fr"][:], c["lr"][:], K["lam_re"][:, 0:1], c["t"][:], ALU.mult, ALU.add))
            link(v.tensor_tensor(c["fr"][:], c["fr"][:], c["den"][:], ALU.mult))
            link(v.tensor_tensor(c["t"][:], c["lr"][:], K["lam_im"][:], ALU.mult))
            link(v.scalar_tensor_tensor(c["fi"][:], c["li"][:], K["lam_re"][:, 0:1], c["t"][:], ALU.mult, ALU.subtract))
            link(v.tensor_tensor(c["fi"][:], c["fi"][:], c["den"][:], ALU.mult))
            link(v.tensor_tensor(c["fi"][:], c["fi"][:], sign[:, 0:1], ALU.mult))
            link(v.tensor_scalar(bb[:], K["b_x2"][:], c["fi"][:, 0:1], None, ALU.mult))
            link(v.scalar_tensor_tensor(bb[:], K["b_x1"][:], c["fr"][:, 0:1], bb[:], ALU.mult, ALU.add))
            v.memset(g1[:], 0.0)
            link(v.memset(g2[:], 0.0))
            for e in range(2):
                for k in range(2):
                    r = slice(64 * e + NP * k, 64 * e + NP * (k + 1))
                    v.tensor_scalar(g1[r, e, :], K["c_x1"][r, :], (2.0, -2.0)[k], None, ALU.mult)
                    v.tensor_scalar(g2[r, e, :], K["c_x2"][r, :], (-2.0, 2.0)[k], None, ALU.mult)
            v.tensor_scalar(dd[:], K["ident"][:], K["ssm_d"][:, 0:1], None, ALU.mult)
            v.memset(dec[:], 1.0)
            v.memset(cc[:, 0:1], 1.0)
            v.memset(ss[:, 0:1], 0.0)
            v.tensor_copy(c["ck"][:], c["cos"][:])
            link(v.tensor_copy(c["sk"][:], c["sin"][:]))
            link(v.tensor_scalar(dec[:], dec[:], c["mag"][:, 0:1], None, ALU.mult))
            n = 1
            while n < S:
                ck, sk = c["ck"], c["sk"]
                v.tensor_scalar(tmp[:, 0:n], ss[:, 0:n], sk[:, 0:1], None, ALU.mult)
                link(v.tensor_scalar(tmp[:, n:2 * n], cc[:, 0:n], sk[:, 0:1], None, ALU.mult))
                v.scalar_tensor_tensor(cc[:, n:2 * n], cc[:, 0:n], ck[:, 0:1], tmp[:, 0:n], ALU.mult, ALU.subtract)
                v.scalar_tensor_tensor(ss[:, n:2 * n], ss[:, 0:n], ck[:, 0:1], tmp[:, n:2 * n], ALU.mult, ALU.add)
                v.tensor_tensor(c["ck2"][:], sk[:], sk[:], ALU.mult)
                link(v.tensor_tensor(c["sk2"][:], ck[:], sk[:], ALU.mult))
                v.scalar_tensor_tensor(ck[:], ck[:], ck[:, 0:1], c["ck2"][:], ALU.mult, ALU.subtract)
                link(v.tensor_scalar(sk[:], c["sk2"][:], 2.0, None, ALU.mult))
                n *= 2
            link(v.tensor_scalar(ss[:], ss[:], sign[:, 1:2], None, ALU.mult))
            ready = link.n
            assert ready == 31 + 1 + 2 + 3 * 9 + 1

            def residual(p, par):
                dve.wait_ge(s_y, p + 1)
                dve.wait_ge(s_xx, p + 1)
                xb = K["x"][:, bass.ds(2 * p * NT, 2 * NT), :]
                v.tensor_tensor(xb, xb, yy[:].rearrange("p e (j d) -> p (e j) d", j=NT), ALU.add).then_inc(s_o, 1)
                dve.wait_ge(s_o, p + 1)
                apart(dve)
                for j in range(2 * NT):
                    ins = v.bn_stats(st6[:, j, :], K["x"][:, 2 * p * NT + j, :])
                ins.then_inc(s_st, 1)
                dve.wait_ge(s_st, 3 * p + 1)
                apart(dve)
                for j in range(2 * NT):
                    ins = v.bn_aggr(mv8[:, j, :], st6[:, j, :])
                ins.then_inc(s_st, 1)
                dve.wait_ge(s_st, 3 * p + 2)
                v.tensor_copy(K["mv"][:, bass.ds(2 * p * NT, 2 * NT), :], mv8[:]).then_inc(s_st, 1)

            def step(p, par):
                last = isinstance(p, int) and p == B // 2 - 1
                dve.wait_ge(s_x, p + 1)
                wait(dve, s_w, p)
                v.tensor_tensor(t1[:], xx[:, 0, :], cc[:], ALU.mult)
                v.tensor_tensor(t2[:], xx[:, 1, :], ss[:], ALU.mult).then_inc(s_r, 1)
                if not last:
                    norm(p + 1, 1 - par)
                dve.wait_ge(s_w, p + 1)
                v.tensor_tensor_scan(wo[:], dec[:], wi[:], 0.0, ALU.mult, ALU.add).then_inc(s_s, 1)
                dve.wait_ge(s_s, 2 * p + 1)
                wait(dve, s_y, p)
                v.tensor_tensor(v1[:], wo[:], cc[:], ALU.mult)
                v.tensor_tensor(v2[:], wo[:], ss[:], ALU.mult).then_inc(s_s, 1)
                if not (isinstance(p, int) and p == 0):
                    residual(p - 1, 1 - par)

            in_fours(dve, step)
            residual(B // 2 - 1, 1)

        @block.scalar
        def _(act):
            a = nc.scalar.activation
            act.wait_ge(s_d, 1)
            a(K["rstd"][:], K["rstd"][:], ACT.Sqrt).then_inc(s_a, 1)
            act.wait_ge(s_d, 5)
            a(r3[:], r3[:], ACT.Sqrt).then_inc(s_a, 1)
            a(c["dt"][:], K["log_step"][:], ACT.Exp).then_inc(s_a, 1)
            act.wait_ge(s_d, 8)
            a(c["mag"][:], c["t"][:], ACT.Exp).then_inc(s_a, 1)
            act.wait_ge(s_d, 17)
            a(c["sin"][:], c["th"][:], ACT.Sin).then_inc(s_a, 1)
            a(c["cos"][:], c["n"][:], ACT.Sin).then_inc(s_a, 1)

            def leave(p, par):
                act.wait_ge(s_t, p + 1)
                wait(act, s_y, p - 1)
                a(ut[:, par], tp[:], ACT.Copy, scale=K["norm_w"][:, 0:1]).then_inc(s_te, 1)

            leave(0, 0)
            act.wait_ge(s_b, 1)
            a(bbt[:], xx[:, 0, 0:P], ACT.Copy).then_inc(s_a, 1)
            in_fours(act, lambda p, par: None if isinstance(p, int) and p == B // 2 - 1 else leave(p + 1, 1 - par))

        @block.gpsimd
        def _(pool):
            pool.wait_ge(s_d, 6)

            def scaled(p, par):
                pool.wait_ge(s_xn, p + 1)
                wait(pool, s_t, p - 1)
                t = bass.ds(2 * p * NT, 2 * NT)
                src = xn[:, par].rearrange("p e j d -> p (e j) d")
                nc.gpsimd.tensor_tensor(un[:, par].rearrange("p e j d -> p (e j) d"), src,
                                        r3[:, t].unsqueeze(2).broadcast_to([P, 2 * NT, P]), ALU.mult).then_inc(s_un, 1)
                nc.gpsimd.tensor_tensor(K["x"][:, t, :], K["x"][:, t, :], src, ALU.add).then_inc(s_xx, 1)

            def step(p, par):
                pool.wait_ge(s_r, p + 1)
                wait(pool, s_s, 2 * p - 1)
                nc.gpsimd.tensor_tensor(wi[:], t1[:], t2[:], ALU.add).then_inc(s_w, 1)
                if not (isinstance(p, int) and p == B // 2 - 1):
                    scaled(p + 1, 1 - par)

            scaled(0, 0)
            in_fours(pool, step)

        @block.tensor
        def _(pe):
            def turn(p, par):
                pe.wait_ge(s_un, p + 1)
                wait(pe, s_te, p)
                for e in range(2):
                    for j in range(NT):
                        mm = nc.tensor.transpose(tp[:, e, j * P:(j + 1) * P], un[:, par, e, j, :], K["ident"][:])
                mm.then_inc(s_t, 1)

            def inputs(p, par):
                pe.wait_ge(s_te, p + 1)
                wait(pe, s_r, p)
                for k in range(2):
                    for e in range(2):
                        mm = nc.tensor.matmul(xx[64 * e:64 * e + 64, k, :], bbt[:, 64 * k:64 * k + 64], ut[:, par, e, :],
                                              start=True, stop=True)
                mm.then_inc(s_x, 1)

            def outputs(p, par):
                pe.wait_ge(s_s, 2 * p + 2)
                wait(pe, s_o, p)
                for e in range(2):
                    for j in range(NT):
                        at = slice(j * P, (j + 1) * P)
                        nc.tensor.matmul(yy[:, e, at], v1[:, at], g1[:, e, :], start=True, stop=False)
                        nc.tensor.matmul(yy[:, e, at], v2[:, at], g2[:, e, :], start=False, stop=False)
                        mm = nc.tensor.matmul(yy[:, e, at], ut[:, par, e, at], dd[:], start=False, stop=True)
                mm.then_inc(s_y, 1)

            turn(0, 0)
            pe.wait_ge(s_d, 31)
            nc.tensor.transpose(xx[:, 0, 0:P], bb[:], K["ident"][:]).then_inc(s_b, 1)
            pe.wait_ge(s_a, 7)

            def step(p, par):
                inputs(p, par)
                if not (isinstance(p, int) and p == B // 2 - 1):
                    turn(p + 1, 1 - par)
                outputs(p, par)

            in_fours(pe, step)

        work.close()
        sem.end()


def program(nc, A, out):
    with ExitStack() as ctx:
        sb = lambda n, s, d=F32: ctx.enter_context(nc.sbuf_tensor("k_" + n, s, d))
        K = {"x": sb("x", [P, T, E]), "mv": sb("mv", [P, T, 2])}
        loads = []

        def load(name, src, shape):
            K[name] = sb(name, shape)
            loads.append((K[name][:], src))

        for n in ("ident", "norm_sel", "later_key"):
            load(n, A["c_" + n], [P, A["c_" + n].shape[1]])
        for n in ("wq", "wk", "wv", "wo"):
            load(n, A[n], [P, E])
        load("gam", A["gam"].partition_broadcast(P), [P, RH])
        K["first"], K["later"] = loads[:], loads
        del loads[:]
        for n in ("iota", "router_rows", "ssm_sign"):
            load(n, A["c_" + n], [P, A["c_" + n].shape[1]])
        load("wqkv", A["wqkv"], [P, 3 * H * DH])
        for n in ("wout_l", "wq_h", "wk_h", "wv_h", "wout_h"):
            load(n, A[n], [P, H * DH])
        load("rt", A["rt"], [P, 2])
        for n in ("ln_w", "ln_b", "gam_h"):
            load(n, A[n], [P, 1])
        load("null_k", A["null_k"], [P, HP])
        load("null_v", A["null_v"], [HP, H * DH])
        load("null_q", A["null_q"], [1, E])
        for n in ("lam_re", "lam_im", "log_step", "ssm_d", "norm_w"):
            load(n, A[n], [P, 1])
        for n in ("b_x1", "b_x2", "c_x1", "c_x2"):
            load(n, A[n], [P, E])
        for n in ("rstd", "r2", "rc"):
            K[n] = sb(n, [P, T])
        for n in ("na", "smax", "m", "sum", "lns"):
            K[n] = sb(n, [2 * B, 1])
        for n in ("srow", "shift"):
            K[n] = sb(n, [2 * B, S])
        K["place"] = sb("place", [P, NT, 2 * B])
        for n in ("negc", "lo", "hi"):
            K[n] = sb(n, [P, RH])
        stage_rbf(nc, K, A)
        coarse_to_fine(nc, K, "f1", True)
        stage_ssm(nc, K)
        coarse_to_fine(nc, K, "f2", False)
        stage_store(nc, K, out)


def coarse_to_fine(nc, K, tag, stats):
    with nc.sbuf_tensor(tag + "_y", [P, T, E], F32) as K["y"]:
        stage_scores(nc, K, tag)
        stage_light(nc, K, tag)
        stage_topk(nc, K, tag)
        stage_heavy(nc, K, tag, stats)


def stage_store(nc, K, out):
    with nc.semaphore("st_out") as so, nc.Block() as block:
        @block.sync
        def _(sp):
            o_d = out.rearrange("(t p) d -> p t d", p=P)
            for q in range(4):
                n = T // 4
                sp.dma_start(o_d[:, q * n:(q + 1) * n, :], K["x"][:, q * n:(q + 1) * n, :]).then_inc(so, 16)
            sp.wait_ge(so, 64)


def lay_out(inp):
    a = {k: np.asarray(v) for k, v in inp.items()}
    r = {}
    r["x"] = a["L0_attn_a_q"].reshape(B * S, E)
    for n in ("Wq", "Wk", "Wv", "Wo"):
        r[n.lower()] = a["L0_attn_a_" + n]
    order = [HEADS[2 * hh + e] * RD + d for d in range(RD) for e in range(2) for hh in range(RH // 2)]
    for n in ("wq", "wk"):
        r[n] = r[n][:, order]
    r["gam"] = a["L0_attn_a_gamma"].reshape(RH)
    def f(n):
        return a["L0_ffn_" + n]

    def chunks(w):
        return w.reshape(-1, P, w.shape[1]).transpose(1, 0, 2).reshape(P, -1)

    r["wqkv"] = f("Wqkv").T
    r["wout_l"] = chunks(f("Wout_l").T)
    r["wq_h"] = f("Wq").T
    kv = f("Wkv").reshape(H, 2, DH, E)
    r["wk_h"] = kv[:, 0].reshape(H * DH, E).T
    r["wv_h"] = kv[:, 1].reshape(H * DH, E).T
    r["wout_h"] = chunks(f("Wout_h").T)
    r["rt"] = np.concatenate([f("rt_q"), f("rt_kv")]).T
    r["ln_w"], r["ln_b"], r["gam_h"] = (f(n).reshape(E, 1) for n in ("ln_w", "ln_b", "gamma"))
    r["null_k"] = f("null_kv")[0].reshape(HP, P).T
    r["null_v"] = np.zeros((HP, HP, 2 * DH), a["L0_ffn_null_kv"].dtype)
    for c in range(HP):
        r["null_v"][c, c] = f("null_kv")[1, 2 * c:2 * c + 2].reshape(2 * DH)
    r["null_v"] = r["null_v"].reshape(HP, H * DH)
    r["null_q"] = f("null_q").reshape(1, E)
    d = lambda n: a["L0_attn_b_" + n]
    four = lambda *v: np.concatenate(v).reshape(P, -1)
    for n in ("Lambda_re", "Lambda_im", "log_step"):
        r[n.replace("Lambda", "lam")] = four(*[d(n)] * 4)
    r["ssm_d"], r["norm_w"] = d("D").reshape(P, 1), d("norm_weight").reshape(P, 1)
    br, bi, cr, ci = d("B_re"), d("B_im"), d("C_re").T, d("C_im").T
    r["b_x1"], r["b_x2"] = four(br, bi, bi, br), four(bi, br, br, bi)
    r["c_x1"], r["c_x2"] = four(cr, ci, cr, ci), four(ci, cr, ci, cr)
    for k, v in host_constants().items():
        r["c_" + k] = v
    return {k: np.ascontiguousarray(v) for k, v in r.items()}


def kernel(**inputs):
    import concourse.bacc as bacc
    from concourse.bass_utils import run_bass_kernel_spmd

    nc = bacc.Bacc("TRN2", target_bir_lowering=False, num_devices=1)
    arrays = lay_out(inputs)
    aps = {n: nc.dram_tensor(n, v.shape, mybir.dt.from_np(v.dtype), kind="ExternalInput").ap()
           for n, v in arrays.items()}
    out = nc.dram_tensor("out", (B * S, E), F32, kind="ExternalOutput").ap()
    program(nc, aps, out)
    r = run_bass_kernel_spmd(nc, [arrays], core_ids=[0])
    return r.results[0]["out"].reshape(B, S, E)
```
